# Optimizing a Trainium2 kernel written in Bass

```python
import numpy as np
import jax
import jax.numpy as jnp

def _softmax(x, axis=-1):
    return jax.nn.softmax(x, axis=axis)

def _gelu(x):
    return jax.nn.gelu(x, approximate=True)

def _silu(x):
    return jax.nn.silu(x)

def _sigmoid(x):
    return jax.nn.sigmoid(x)

def _layernorm(x, axis=-1, eps=1e-05):
    m = jnp.mean(x, axis=axis, keepdims=True)
    v = jnp.var(x, axis=axis, keepdims=True)
    return (x - m) / jnp.sqrt(v + eps)

def _scatter_add(tgt, idx, src, axis=0):
    return tgt.at[idx].add(src)

def _segment_sum(src, seg, n):
    return jax.ops.segment_sum(src, seg, n)
kernel_name = 'mk_xattn_seq_d2_seqx_r4_41b850'

def setup_inputs(seed: int=0):
    np.random.seed(seed)
    _w = jnp.asarray

    def _rec_inputs():
        import jax
        import jax.numpy as jnp
        _rk = jax.random.key(seed)
        x = -0.0002928 + 1 * jax.random.normal(jax.random.fold_in(_rk, 1), (8, 512, 256), jnp.float32)
        _lenS = 512 - jax.random.randint(jax.random.fold_in(_rk, 7), (8,), 0, max(1, 512 // 4) + 1, jnp.int32)
        _lenS2 = 1024 - jax.random.randint(jax.random.fold_in(_rk, 8), (8,), 0, max(1, 1024 // 4) + 1, jnp.int32)
        _ctx_1024P = jax.random.normal(jax.random.fold_in(_rk, 11), (8, 16, 256), jnp.float32)
        _ctx_1024c = jax.random.dirichlet(jax.random.fold_in(_rk, 511), 0.3 * jnp.ones((16,), jnp.float32), (8, 1024))
        _ctx_1024t = jnp.einsum('bsk,bkd->bsd', _ctx_1024c, _ctx_1024P)
        _ctx_1024t = _ctx_1024t * jax.lax.rsqrt(jnp.mean(jnp.square(_ctx_1024t)) + 1e-12) * 0.953939
        ctx_1024 = -1.39393e-06 + 0.999914 * (_ctx_1024t + 0.3 * jax.random.normal(jax.random.fold_in(_rk, 611), (8, 1024, 256), jnp.float32))
        return (x, ctx_1024)
    x, ctx_1024 = _rec_inputs()

    def _L0_xattn_setup():
        import jax, jax.numpy as jnp
        import numpy as np
        D_MODEL = 256
        N_HEADS = 16
        D_K = D_MODEL // N_HEADS
        LN_EPS = 1e-05

        def _attention(query, key_value, W_qkv, b_qkv, W_o, b_o, ln_gamma, ln_beta):
            B, Sq, _ = query.shape
            Skv = key_value.shape[1]
            Wq, Wk, Wv = (W_qkv[:D_MODEL], W_qkv[D_MODEL:2 * D_MODEL], W_qkv[2 * D_MODEL:])
            bq, bk, bv = (b_qkv[:D_MODEL], b_qkv[D_MODEL:2 * D_MODEL], b_qkv[2 * D_MODEL:])
            Q = (query @ Wq.T + bq).reshape(B, Sq, N_HEADS, D_K).transpose(0, 2, 1, 3)
            K = (key_value @ Wk.T + bk).reshape(B, Skv, N_HEADS, D_K).transpose(0, 2, 1, 3)
            V = (key_value @ Wv.T + bv).reshape(B, Skv, N_HEADS, D_K).transpose(0, 2, 1, 3)
            scores = jnp.einsum('bhqd,bhkd->bhqk', Q.astype(jnp.float32), K.astype(jnp.float32))
            scores = scores / np.sqrt(D_K)
            attn = jax.nn.softmax(scores, axis=-1)
            context = jnp.einsum('bhqk,bhkd->bhqd', attn, V.astype(jnp.float32)).astype(query.dtype)
            context = context.transpose(0, 2, 1, 3).reshape(B, Sq, D_MODEL)
            output = context @ W_o.T + b_o
            x = output + query
            mu = jnp.mean(x, axis=-1, keepdims=True)
            var = jnp.mean(jnp.square(x - mu), axis=-1, keepdims=True)
            return (x - mu) / jnp.sqrt(var + LN_EPS) * ln_gamma + ln_beta
        key = jax.random.key(seed)
        ks = jax.random.split(key, 8)
        B, Sq, Skv = (2, 512, 512)
        scale = 1.0 / np.sqrt(D_MODEL)
        return {'query': jax.random.normal(ks[0], (B, Sq, D_MODEL), dtype=jnp.float32), 'key_value': jax.random.normal(ks[1], (B, Skv, D_MODEL), dtype=jnp.float32), 'W_qkv': jax.random.normal(ks[2], (3 * D_MODEL, D_MODEL), dtype=jnp.float32) * scale, 'b_qkv': jax.random.normal(ks[3], (3 * D_MODEL,), dtype=jnp.float32) * 0.01, 'W_o': jax.random.normal(ks[4], (D_MODEL, D_MODEL), dtype=jnp.float32) * scale, 'b_o': jax.random.normal(ks[5], (D_MODEL,), dtype=jnp.float32) * 0.01, 'ln_gamma': jnp.ones((D_MODEL,), dtype=jnp.float32), 'ln_beta': jnp.zeros((D_MODEL,), dtype=jnp.float32)}
    _L0_xattn_all = _L0_xattn_setup()
    _L0_xattn_in = {k: v for k, v in _L0_xattn_all.items() if k in ('W_qkv', 'b_qkv', 'W_o', 'b_o', 'ln_gamma', 'ln_beta')}
    del _L0_xattn_all

    def _L1_xattn_setup():
        import jax, jax.numpy as jnp
        import numpy as np
        D_MODEL = 256
        NUM_HEADS = 16
        HEAD_DIM = D_MODEL // NUM_HEADS
        SCALE = HEAD_DIM ** (-0.5)
        LN_EPS = 1e-05
        Q_EPS = 1e-05

        def bit_quant(W):
            gamma = jnp.mean(jnp.abs(W))
            Wq = jnp.clip(jnp.round(W / (gamma + Q_EPS)), -1.0, 1.0) * gamma
            return W + jax.lax.stop_gradient(Wq - W)

        def layer_norm(x, gamma, beta):
            mu = jnp.mean(x, axis=-1, keepdims=True)
            var = jnp.mean(jnp.square(x - mu), axis=-1, keepdims=True)
            return (x - mu) * jax.lax.rsqrt(var + LN_EPS) * gamma + beta
        key = jax.random.key(seed)
        ks = jax.random.split(key, 8)
        B, T, T_ctx, C = (4, 256, 512, D_MODEL)
        w_std = C ** (-0.5)
        return {'x': jax.random.normal(ks[0], (B, T, C), jnp.float32), 'context': jax.random.normal(ks[1], (B, T_ctx, C), jnp.float32), 'Wq': jax.random.normal(ks[2], (C, C), jnp.float32) * w_std, 'bq': jnp.zeros((C,), jnp.float32), 'Wk': jax.random.normal(ks[3], (C, C), jnp.float32) * w_std, 'bk': jnp.zeros((C,), jnp.float32), 'Wv': jax.random.normal(ks[4], (C, C), jnp.float32) * w_std, 'bv': jnp.zeros((C,), jnp.float32), 'Wo': jax.random.normal(ks[5], (C, C), jnp.float32) * w_std, 'bo': jnp.zeros((C,), jnp.float32), 'ln_gamma': jnp.ones((C,), jnp.float32), 'ln_beta': jnp.zeros((C,), jnp.float32)}
    _L1_xattn_all = _L1_xattn_setup()
    _L1_xattn_in = {k: v for k, v in _L1_xattn_all.items() if k in ('Wq', 'bq', 'Wk', 'bk', 'Wv', 'bv', 'Wo', 'bo', 'ln_gamma', 'ln_beta')}
    del _L1_xattn_all
    return {'x': x, 'ctx_1024': ctx_1024, 'L0_xattn_W_qkv': _L0_xattn_in['W_qkv'], 'L0_xattn_b_qkv': _L0_xattn_in['b_qkv'], 'L0_xattn_W_o': _L0_xattn_in['W_o'], 'L0_xattn_b_o': _L0_xattn_in['b_o'], 'L0_xattn_ln_gamma': _L0_xattn_in['ln_gamma'], 'L0_xattn_ln_beta': _L0_xattn_in['ln_beta'], 'L1_xattn_Wq': _L1_xattn_in['Wq'], 'L1_xattn_bq': _L1_xattn_in['bq'], 'L1_xattn_Wk': _L1_xattn_in['Wk'], 'L1_xattn_bk': _L1_xattn_in['bk'], 'L1_xattn_Wv': _L1_xattn_in['Wv'], 'L1_xattn_bv': _L1_xattn_in['bv'], 'L1_xattn_Wo': _L1_xattn_in['Wo'], 'L1_xattn_bo': _L1_xattn_in['bo'], 'L1_xattn_ln_gamma': _L1_xattn_in['ln_gamma'], 'L1_xattn_ln_beta': _L1_xattn_in['ln_beta']}

def reference(x, ctx_1024, L0_xattn_W_qkv, L0_xattn_b_qkv, L0_xattn_W_o, L0_xattn_b_o, L0_xattn_ln_gamma, L0_xattn_ln_beta, L1_xattn_Wq, L1_xattn_bq, L1_xattn_Wk, L1_xattn_bk, L1_xattn_Wv, L1_xattn_bv, L1_xattn_Wo, L1_xattn_bo, L1_xattn_ln_gamma, L1_xattn_ln_beta):
    import jax
    import jax.numpy as jnp

    def _L0_xattn_ref(query, key_value, W_qkv, b_qkv, W_o, b_o, ln_gamma, ln_beta):
        import jax, jax.numpy as jnp
        import numpy as np
        D_MODEL = 256
        N_HEADS = 16
        D_K = D_MODEL // N_HEADS
        LN_EPS = 1e-05

        def _attention(query, key_value, W_qkv, b_qkv, W_o, b_o, ln_gamma, ln_beta):
            B, Sq, _ = query.shape
            Skv = key_value.shape[1]
            Wq, Wk, Wv = (W_qkv[:D_MODEL], W_qkv[D_MODEL:2 * D_MODEL], W_qkv[2 * D_MODEL:])
            bq, bk, bv = (b_qkv[:D_MODEL], b_qkv[D_MODEL:2 * D_MODEL], b_qkv[2 * D_MODEL:])
            Q = (query @ Wq.T + bq).reshape(B, Sq, N_HEADS, D_K).transpose(0, 2, 1, 3)
            K = (key_value @ Wk.T + bk).reshape(B, Skv, N_HEADS, D_K).transpose(0, 2, 1, 3)
            V = (key_value @ Wv.T + bv).reshape(B, Skv, N_HEADS, D_K).transpose(0, 2, 1, 3)
            scores = jnp.einsum('bhqd,bhkd->bhqk', Q.astype(jnp.float32), K.astype(jnp.float32))
            scores = scores / np.sqrt(D_K)
            attn = jax.nn.softmax(scores, axis=-1)
            context = jnp.einsum('bhqk,bhkd->bhqd', attn, V.astype(jnp.float32)).astype(query.dtype)
            context = context.transpose(0, 2, 1, 3).reshape(B, Sq, D_MODEL)
            output = context @ W_o.T + b_o
            x = output + query
            mu = jnp.mean(x, axis=-1, keepdims=True)
            var = jnp.mean(jnp.square(x - mu), axis=-1, keepdims=True)
            return (x - mu) / jnp.sqrt(var + LN_EPS) * ln_gamma + ln_beta
        return _attention(query, key_value, W_qkv, b_qkv, W_o, b_o, ln_gamma, ln_beta)

    def _L1_xattn_ref(x, context, Wq, bq, Wk, bk, Wv, bv, Wo, bo, ln_gamma, ln_beta):
        import jax, jax.numpy as jnp
        import numpy as np
        D_MODEL = 256
        NUM_HEADS = 16
        HEAD_DIM = D_MODEL // NUM_HEADS
        SCALE = HEAD_DIM ** (-0.5)
        LN_EPS = 1e-05
        Q_EPS = 1e-05

        def bit_quant(W):
            gamma = jnp.mean(jnp.abs(W))
            Wq = jnp.clip(jnp.round(W / (gamma + Q_EPS)), -1.0, 1.0) * gamma
            return W + jax.lax.stop_gradient(Wq - W)

        def layer_norm(x, gamma, beta):
            mu = jnp.mean(x, axis=-1, keepdims=True)
            var = jnp.mean(jnp.square(x - mu), axis=-1, keepdims=True)
            return (x - mu) * jax.lax.rsqrt(var + LN_EPS) * gamma + beta
        B, T, C = x.shape
        T_ctx = context.shape[1]
        residual = x
        xn = layer_norm(x, ln_gamma, ln_beta)
        q = xn @ bit_quant(Wq).T + bq
        k = context @ bit_quant(Wk).T + bk
        v = context @ bit_quant(Wv).T + bv
        q = q.reshape(B, T, NUM_HEADS, HEAD_DIM)
        k = k.reshape(B, T_ctx, NUM_HEADS, HEAD_DIM)
        v = v.reshape(B, T_ctx, NUM_HEADS, HEAD_DIM)
        scores = jnp.einsum('bqhd,bkhd->bhqk', q, k) * SCALE
        probs = jax.nn.softmax(scores, axis=-1)
        out = jnp.einsum('bhqk,bkhd->bqhd', probs, v).reshape(B, T, C)
        return residual + (out @ bit_quant(Wo).T + bo)
    x = _L0_xattn_ref(x, ctx_1024, L0_xattn_W_qkv, L0_xattn_b_qkv, L0_xattn_W_o, L0_xattn_b_o, L0_xattn_ln_gamma, L0_xattn_ln_beta)
    x = _L1_xattn_ref(x, ctx_1024, L1_xattn_Wq, L1_xattn_bq, L1_xattn_Wk, L1_xattn_bk, L1_xattn_Wv, L1_xattn_bv, L1_xattn_Wo, L1_xattn_bo, L1_xattn_ln_gamma, L1_xattn_ln_beta)
    return x

_drawn_inputs = setup_inputs


def setup_inputs(seed=0):
    import zlib

    import numpy as np

    out = dict(_drawn_inputs(seed))
    spreads = {'L0_xattn_ln_gamma': (1.0, 0.2),
     'L0_xattn_ln_beta': (0.0, 0.1),
     'L1_xattn_bq': (0.0, 0.8),
     'L1_xattn_bk': (0.0, 0.8),
     'L1_xattn_bv': (0.0, 0.1),
     'L1_xattn_bo': (0.0, 0.1),
     'L1_xattn_ln_gamma': (1.0, 0.6),
     'L1_xattn_ln_beta': (0.0, 0.8)}
    factors = {'L0_xattn_b_qkv': 6.668, 'L0_xattn_b_o': 6.335}
    for name, (base, spread) in spreads.items():
        noise = np.random.default_rng([zlib.crc32(name.encode()), seed]).standard_normal(out[name].shape)
        drawn = base * np.exp(spread * noise) if base else spread * noise
        out[name] = jnp.asarray(drawn.astype(out[name].dtype))
    for name, factor in factors.items():
        out[name] = (out[name] * factor).astype(out[name].dtype)
    return out
```

```python
from contextlib import ExitStack

import concourse.bass as bass
from concourse import mybir

ALU = mybir.AluOpType
ACT = mybir.ActivationFunctionType
AX = mybir.AxisListType
F32 = mybir.dt.float32
BF16 = mybir.dt.bfloat16

P = 128
B, SQ, SK, D, H = 8, 512, 1024, 256, 16
DH = D // H
GH = 4
NG = H // GH
QB = SQ // P
KB = SK // P
NC = D // P
BANK = 512
KH = SK // BANK
K_PART = (0, 1, 2, 0, 1, 0)
Q_PART = (0, 0, 0, 1, 1, 2)
NT = len(K_PART)
ROWS = NT * DH
SROWS = ROWS + 2
LN_EPS = 1e-5
QUANT_EPS = 1e-5
SCALE = float(DH) ** -0.5
HALF_TILES = KH + 1
TILES = NC * HALF_TILES
NEXT_MAX = (6, 6, 5, 5, 5, 5, 0, 0)
Q, K, V, O = range(4)


def prep_items(layer):
    rows = [("xnT", c) for c in range(NC)] if layer == 1 else []
    return (rows + [("k", 0, 0), ("k", 0, 1), ("q", 0), ("v", 0)],
            [("v", 1), ("v", 2)],
            [("k", 1, 0), ("k", 1, 1), ("q", 1), ("v", 3)],
            [])


def max_items(g):
    return [("max", g, h, qb, kh) for h in range(GH) for qb in range(QB) for kh in range(KH)]


class Unit:

    def __init__(self, index, layer, batch, w0, parity, before, after):
        self.index, self.layer, self.batch = index, layer, batch
        self.w0, self.parity, self.before, self.after = w0, parity, before, after
        self.plan = {}
        for g in range(NG):
            todo = max_items((g + 1) % NG) if g + 1 < NG or after is not None else []
            late = [("maxT", (g + 1) % NG)] if todo else []
            if after is not None:
                late += prep_items(after)[g]
            if g == 1 and before is not None:
                late += [("o", 0), ("o", 1)]
            for kb, n in enumerate(NEXT_MAX):
                self.plan[g, kb], todo = todo[:n], todo[n:]
            half = (len(late) + 1) // 2
            self.plan[g, KB - 2] += late[:half]
            self.plan[g, KB - 1] += late[half:]
        self.order = [item for at in sorted(self.plan) for item in self.plan[at]]
        self.number = {item: n for n, item in enumerate(self.order)}

    def work(self, item):
        return self.w0 + self.number[item]

    def slot(self, item):
        return (self.parity + self.number[item]) % 2


class Prologue(Unit):

    def __init__(self):
        self.index, self.layer, self.batch, self.w0, self.parity = -1, 0, -1, 0, 0
        self.before, self.after = None, 0
        self.order = [i for group in prep_items(0) for i in group] + max_items(0) + [("maxT", 0)]
        self.number = {item: n for n, item in enumerate(self.order)}


def plan_units():
    prologue = Prologue()
    w = len(prologue.order)
    entries = []
    for layer in range(2):
        for batch in (0, 1, B - 1):
            before = None if layer == 0 and batch == 0 else (0 if batch == 0 else layer)
            after = (1 if layer == 0 else None) if batch == B - 1 else layer
            n = len(Unit(0, layer, batch, 0, 0, before, after).order)
            entries.append((layer, batch, w, n, before, after))
            w += n * (B - 2 if batch == 1 else 1)
            assert batch != 1 or n % 2 == 0
    return prologue, entries


def xattn_two_layers(nc, a, out):
    x_in = {0: a["x"], 1: nc.dram_tensor("layer0_out", (B, SQ, D), F32, kind="Internal").ap()}
    x_out = {0: x_in[1], 1: out}
    prologue, entries = plan_units()

    def run_units(eng, body):
        for layer, batch, w, n, before, after in entries:
            if batch == 1:
                with eng.Fori(1, B - 1) as i:
                    body(Unit(i + layer * B if layer else i, layer, i, (i - 1) * n + w, w % 2, before, after))
            else:
                body(Unit(layer * B + batch, layer, batch, w, w % 2, before, after))

    with ExitStack() as ctx:
        def sb(name, shape, dt=F32):
            return ctx.enter_context(nc.sbuf_tensor(name, shape, dt))

        def sem(name):
            return ctx.enter_context(nc.semaphore(name))

        k6 = sb("k6", [P, H, SK], BF16)
        q6 = sb("q6", [P, H, SQ], BF16)
        vx = sb("vx", [P, NG, KB, GH, 2 * DH])
        probs = sb("probs", [P, 2, GH, SQ])
        ctx_t = sb("ctx_t", [P, NC, SK])
        x_t = sb("x_t", [P, NC, SQ])
        full = sb("full", [P, 2, BANK])
        rest = sb("rest", [P, BANK])
        ks = sb("ks", [P, NC, 3, SK], BF16)
        qs = sb("qs", [P, NC, 3, SQ], BF16)
        vs = sb("vs", [P, KB, D])
        rows = sb("rows", [P, QB, D])
        rows_n = sb("rows_n", [P, QB, D])
        o_raw = sb("o_raw", [P, 2, SQ])
        num = sb("num", [P, SQ])
        den = sb("den", [P, SQ])
        rden = sb("rden", [P, SQ])
        attn_t = sb("attn_t", [P, NC, SQ])
        res = sb("res", [P, QB, D])
        resb = sb("resb", [P, QB, D])
        y = sb("y", [P, QB, D])
        fin = sb("fin", [P, QB, D])
        negmax = sb("negmax", [P, KH, GH * QB])
        nm = sb("nm", [P, GH * QB])
        nm_parts = sb("nm_parts", [P, 2, GH * QB], BF16)
        nm_t = sb("nm_t", [2 * GH * QB, P], BF16)
        stats = sb("stats", [P, 2, QB, 6])
        mv = sb("mv", [P, 2, QB, 2])
        var = sb("var", [P, 2, QB])
        rstd = sb("rstd", [P, 2, QB])
        wts = sb("wts", [P, 2, 4, NC, D])
        absum = sb("absum", [P, 4])
        gam = sb("gam", [P, 4])
        thr = sb("thr", [P, 2, 4])
        tern = sb("tern", [P, 2, NC, D])
        ones = sb("ones", [P, P])
        eye = sb("eye", [P, P])
        eyeb = sb("eyeb", [P, P], BF16)
        mhalf = sb("mhalf", [P, QB])
        bqk = sb("bqk", [P, 2, 2, NC])
        bv = sb("bv", [P, 2, D])
        bo = sb("bo", [P, 2, D])
        ln0 = sb("ln0", [P, 2, D])
        ln1 = sb("ln1", [P, 2, NC])

        ps = ctx.enter_context(nc.psum_tensor("ps", [P, 2, 2 * BANK], F32))
        pw = ctx.enter_context(nc.psum_tensor("pw", [P, 2, BANK], F32))
        po = ctx.enter_context(nc.psum_tensor("po", [P, 2, BANK], F32))

        const_in = sem("const_in")
        wts_in = [sem(f"wts_in{l}") for l in range(2)]
        ctx_in = sem("ctx_in")
        x_t_in = sem("x_t_in")
        rows_in = sem("rows_in")
        res_in = sem("res_in")
        restacked = [sem(f"restacked{g}") for g in range(NG)]
        max_placed = sem("max_placed")
        o_moved = [sem(f"o_moved{p}") for p in range(2)]
        stored = sem("stored")
        consts_set = sem("consts_set")
        ones_set = sem("ones_set")
        abs_summed = sem("abs_summed")
        total_ready = sem("total_ready")
        quant_link = sem("quant_link")
        work_full = sem("work_full")
        work_done = sem("work_done")
        scores_full = sem("scores_full")
        probs_ready = sem("probs_ready")
        pv_done = sem("pv_done")
        o_copied = sem("o_copied")
        high_done = sem("high_done")
        split_link = sem("split_link")
        split_done = sem("split_done")
        v_placed = sem("v_placed")
        max_link = sem("max_link")
        max_split = sem("max_split")
        attn_link = sem("attn_link")
        attn_ready = sem("attn_ready")
        resb_ready = sem("resb_ready")
        stat_link = sem("stat_link")
        var_ready = sem("var_ready")
        norm_link = sem("norm_link")
        fin_ready = sem("fin_ready")
        rstat_link = sem("rstat_link")
        rvar_ready = sem("rvar_ready")
        rnorm_link = sem("rnorm_link")
        rows_ready = sem("rows_ready")

        settled = {e: sem(f"settled_{e}") for e in ("sp", "dve", "pool")}

        def settle(eng, name):
            eng.sem_inc(settled[name], 1)

        def wait(eng, sem, count):
            if not isinstance(count, int) or count > 0:
                eng.wait_ge(sem, count)
                if eng is nc.sync and not isinstance(count, int):
                    settle(eng, "sp")

        block = ctx.enter_context(nc.Block())
        N_CONST = 9
        W_LAST = entries[-1][2] + entries[-1][3]
        W_END = W_LAST + 2

        def rows_of(dram, batch):
            return dram[batch].rearrange("(t p) d -> p t d", p=P)

        @block.sync
        def _(sp):
            def load_inputs(layer, batch):
                sp.dma_start(ctx_t[:], a["ctxT"][batch].rearrange("(c p) n -> p c n", p=P)).then_inc(ctx_in, 16)
                if layer == 0:
                    sp.dma_start(x_t[:], a["xT"][batch].rearrange("(c p) n -> p c n", p=P)).then_inc(x_t_in, 16)

            def restack(index, g):
                half, lane = g // 2, 64 * (g % 2)
                wait(sp, split_done, index * TILES + (half + 1) * HALF_TILES)
                for t in range(NT):
                    sp.dma_start(k6[DH * t:DH * t + DH, GH * g:GH * g + GH, :],
                                 ks[lane:lane + 64, half, K_PART[t], :]).then_inc(restacked[g], 16)
                    sp.dma_start(q6[DH * t:DH * t + DH, GH * g:GH * g + GH, :],
                                 qs[lane:lane + 64, half, Q_PART[t], :]).then_inc(restacked[g], 16)

            def place_max(u, g):
                wait(sp, work_done, u.work(("maxT", g)) + 1)
                sp.dma_start(q6[ROWS:SROWS, GH * g:GH * g + GH, :], nm_t[:, :]).then_inc(max_placed, 16)

            def move_o(index, g):
                wait(sp, o_copied, index * NG + g + 1)
                wait(sp, attn_ready, index * NC + g // 2)
                lane = 64 * (g % 2)
                for c, t in ((0, num), (1, den)):
                    sp.dma_start(t[lane:lane + 64, :], o_raw[c:P:2, g % 2, :]).then_inc(o_moved[g % 2], 16)

            def load_residual(index, layer, batch):
                if layer == 1:
                    wait(sp, stored, batch * 16 + 16)
                sp.dma_start(res[:], rows_of(x_in[layer], batch)).then_inc(res_in, 16)

            load_inputs(0, 0)
            sp.dma_start(bqk[:].rearrange("p l k c -> p (l k c)"), a["bqk"]).then_inc(const_in, 16)
            sp.dma_start(eye[:], a["eye"]).then_inc(const_in, 16)
            for l in range(2):
                sp.dma_start(bv[:, l, :], a["bv"][l:l + 1, :].to_broadcast([P, D])).then_inc(const_in, 16)
                sp.dma_start(bo[:, l, :], a["bo"][l:l + 1, :].to_broadcast([P, D])).then_inc(const_in, 16)
                sp.dma_start(ln0[:, l, :], a["ln0"][l:l + 1, :].to_broadcast([P, D])).then_inc(const_in, 16)
            sp.dma_start(ln1[:].rearrange("p k c -> p (k c)"), a["ln1"]).then_inc(const_in, 16)
            for g in range(NG):
                restack(0, g)
            place_max(prologue, 0)

            def unit(u):
                U = u.index
                wait(sp, work_done, u.w0)
                if u.after is not None:
                    next_batch = 0 if u.after != u.layer else u.batch + 1
                    load_inputs(u.after, next_batch)
                    if u.after == 1:
                        if u.layer == 1:
                            wait(sp, rows_ready, U - (B - 1))
                        wait(sp, stored, next_batch * 16 + 16)
                        sp.dma_start(rows[:], rows_of(x_in[1], next_batch)).then_inc(rows_in, 16)
                if u.before is not None:
                    last_batch = B - 1 if u.before != u.layer else u.batch - 1
                    move_o(U - 1, NG - 1)
                    wait(sp, scores_full, U * (NG * KB * 2))
                    restack(U, NG - 1)
                    load_residual(U - 1, u.before, last_batch)
                for g in range(NG):
                    if g > 0:
                        move_o(U, g - 1)
                        if u.after is not None:
                            wait(sp, scores_full, U * (NG * KB * 2) + g * KB * 2)
                            restack(U + 1, g - 1)
                    if g + 1 < NG or u.after is not None:
                        place_max(u, (g + 1) % NG)
                if u.before is not None:
                    if u.before == 0:
                        wait(sp, fin_ready, U)
                    else:
                        wait(sp, work_done, u.work(("o", 1)) + 1)
                    sp.dma_start(rows_of(x_out[u.before], last_batch), fin[:]).then_inc(stored, 16)
                    wait(sp, stored, U * 16)

            run_units(sp, unit)
            move_o(2 * B - 1, NG - 1)
            wait(sp, work_done, W_LAST)
            load_residual(2 * B - 1, 1, B - 1)
            wait(sp, work_done, W_END)
            sp.dma_start(rows_of(out, B - 1), fin[:]).then_inc(stored, 16)
            wait(sp, stored, 2 * B * 16)

        @block.tensor
        def _(pe):
            def start_work(u, item):
                wait(pe, work_done, u.work(item) - 1)
                return pw[:, u.slot(item), :]

            def o_proj(dst, layer, o):
                for j in range(2):
                    qb = 2 * o + j
                    for c in range(NC):
                        mm = nc.tensor.matmul(dst[:, D * j:D * j + D], attn_t[:, c, P * qb:P * qb + P],
                                              wts[:, layer, O, c, :], start=(c == 0), stop=(c == NC - 1))
                return mm

            def work(u, item):
                dst = start_work(u, item)
                kind, nl, U = item[0], u.after, u.index
                if kind == "max":
                    _, g, h, qb, kh = item
                    if (h, qb, kh) == (0, 0, 0):
                        pe.wait_ge(restacked[g], (U + (g == 0)) * (2 * NT * 16) + 2 * NT * 16)
                    s = GH * g + h
                    mm = nc.tensor.matmul(dst, q6[0:ROWS, s, P * qb:P * qb + P],
                                          k6[0:ROWS, s, BANK * kh:BANK * kh + BANK], start=True, stop=True)
                elif kind == "maxT":
                    pe.wait_ge(max_split, U * NG + (item[1] or NG) + 1)
                    mm = nc.tensor.transpose(dst.bitcast(BF16)[0:2 * GH * QB, 0:P],
                                             nm_parts[:].rearrange("p k n -> p (k n)"), eyeb[:])
                elif kind == "xnT":
                    pe.wait_ge(rows_ready, U - (B - 1) + 1)
                    for qb in range(QB):
                        mm = nc.tensor.transpose(dst[:, P * qb:P * qb + P],
                                                 rows_n[:, qb, P * item[1]:P * item[1] + P], eye[:])
                elif kind == "k":
                    _, half, kh = item
                    if (half, kh) == (0, 0):
                        pe.wait_ge(ctx_in, U * 16 + 32)
                    for c in range(NC):
                        mm = nc.tensor.matmul(dst, wts[:, nl, K, c, P * half:P * half + P],
                                              ctx_t[:, c, BANK * kh:BANK * kh + BANK],
                                              start=(c == 0), stop=(c == NC - 1))
                elif kind == "q":
                    half = item[1]
                    if half == 0:
                        if nl == 0:
                            pe.wait_ge(x_t_in, U * 16 + 32)
                        else:
                            pe.wait_ge(work_done, u.work(("xnT", NC - 1)) + 1)
                    for c in range(NC):
                        mm = nc.tensor.matmul(dst, wts[:, nl, Q, c, P * half:P * half + P], x_t[:, c, :],
                                              start=(c == 0), stop=(c == NC - 1))
                elif kind == "v":
                    for j in range(2):
                        kb = 2 * item[1] + j
                        for c in range(NC):
                            mm = nc.tensor.matmul(dst[:, D * j:D * j + D], ctx_t[:, c, P * kb:P * kb + P],
                                                  wts[:, nl, V, c, :], start=(c == 0), stop=(c == NC - 1))
                else:
                    if item[1] == 0:
                        pe.wait_ge(attn_ready, U * NC)
                    mm = o_proj(dst, u.before, item[1])
                mm.then_inc(work_full, 1)

            def scores(u, g, kb, p):
                step = u.index * (NG * KB) + (g * KB + kb)
                if kb == 0 and p == 0:
                    pe.wait_ge(max_placed, (u.index * NG + g + 1) * 16)
                wait(pe, probs_ready, step * 2 + (p - 1))
                for j in range(2):
                    s = GH * g + 2 * p + j
                    mm = nc.tensor.matmul(ps[:, p, BANK * j:BANK * j + BANK],
                                          k6[0:SROWS, s, P * kb:P * kb + P], q6[0:SROWS, s, :],
                                          start=True, stop=True)
                mm.then_inc(scores_full, 1)

            def values(index, g, kb):
                if kb == 0:
                    pe.wait_ge(v_placed, index * NG + g + 1)
                    wait(pe, o_copied, index * NG + (g - 1))
                pe.wait_ge(probs_ready, index * (NG * KB * 2) + (g * KB + kb + 1) * 2)
                for h in range(GH):
                    mm = nc.tensor.matmul(po[32 * h:32 * h + 32, g % 2, :], vx[:, g, kb, h, :],
                                          probs[:, kb % 2, h, :], start=(kb == 0), stop=(kb == KB - 1))
                mm.then_inc(pv_done, 1)

            pe.wait_ge(const_in, N_CONST * 16)
            pe.wait_ge(wts_in[0], 4 * 16)
            pe.wait_ge(consts_set, 1)
            for item in prologue.order:
                work(prologue, item)
            pe.wait_ge(abs_summed, 4)
            nc.tensor.matmul(po[:, 1, 0:4], ones[:], absum[:], start=True, stop=True).then_inc(total_ready, 1)

            def unit(u):
                for g in range(NG):
                    for kb in range(KB):
                        items = u.plan[g, kb]
                        third = (len(items) + 2) // 3
                        scores(u, g, kb, 0)
                        for item in items[:third]:
                            work(u, item)
                        scores(u, g, kb, 1)
                        for item in items[third:2 * third]:
                            work(u, item)
                        if kb > 0:
                            values(u.index, g, kb - 1)
                        elif g > 0:
                            values(u.index, g - 1, KB - 1)
                        elif u.before is not None:
                            values(u.index - 1, NG - 1, KB - 1)
                        for item in items[2 * third:]:
                            work(u, item)

            run_units(pe, unit)
            values(2 * B - 1, NG - 1, KB - 1)
            pe.wait_ge(attn_ready, 2 * B * NC)
            for o in range(2):
                pe.wait_ge(work_done, W_LAST + o - 1)
                o_proj(pw[:, (W_LAST + o) % 2, :], 1, o).then_inc(work_full, 1)

        @block.scalar
        def _(act):
            for l in range(2):
                for m in range(4):
                    act.dma_start(wts[:, l, m, :, :], a["wts"][l, m].rearrange("(c p) n -> p c n", p=P)
                                  ).then_inc(wts_in[l], 16)

            def copy_o(index, g):
                act.wait_ge(pv_done, index * (NG * KB) + (g + 1) * KB)
                wait(act, o_moved[g % 2], (index * NC + g // 2) * 32)
                nc.scalar.copy(o_raw[:, g % 2, :], po[:, g % 2, :]).then_inc(o_copied, 1)

            def unit(u):
                for g in range(NG):
                    for kb in range(KB):
                        step = u.index * (NG * KB) + (g * KB + kb)
                        wait(act, pv_done, step - 1)
                        for p in range(2):
                            act.wait_ge(scores_full, step * 2 + (p + 1))
                            nc.scalar.activation(probs[:, kb % 2, 2 * p:2 * p + 2, :].rearrange("p h n -> p (h n)"),
                                                 ps[:, p, :], ACT.Exp, scale=SCALE).then_inc(probs_ready, 1)
                        if kb == 0 and g > 0:
                            copy_o(u.index, g - 1)
                        elif kb == 0 and u.before is not None:
                            copy_o(u.index - 1, NG - 1)

            run_units(act, unit)
            copy_o(2 * B - 1, NG - 1)

        @block.vector
        def _(dve):
            nc.vector.memset(ones[:], 1.0)
            nc.vector.memset(mhalf[:], -0.5)
            nc.vector.memset(k6[ROWS:SROWS, :, :], 1.0)
            nc.vector.memset(vx[:, :, :, :, 1:2 * DH:2], 1.0)
            dve.wait_ge(const_in, N_CONST * 16)
            nc.vector.tensor_copy(eyeb[:], eye[:]).then_inc(consts_set, 1)

            def work(u, item):
                src = pw[:, u.slot(item), :]
                kind, nl, U, n = item[0], u.after, u.index, u.work(item)
                dve.wait_ge(work_full, n + 1)
                if kind == "max":
                    _, g, h, qb, kh = item
                    nc.vector.tensor_reduce(negmax[:, kh, QB * h + qb:QB * h + qb + 1], src, AX.X, ALU.max,
                                            negate=True).then_inc(work_done, 1)
                    if (h, qb, kh) == (GH - 1, QB - 1, KH - 1):
                        split_max(u, g, n + 1)
                elif kind == "maxT":
                    wait(dve, max_placed, (U * NG + (item[1] or NG)) * 16)
                    nc.vector.tensor_copy(nm_t[:], src.bitcast(BF16)[0:2 * GH * QB, 0:P]).then_inc(work_done, 1)
                elif kind == "xnT":
                    c = item[1]
                    nc.vector.tensor_scalar(x_t[:, c, :], src, ln1[:, 0, c:c + 1], ln1[:, 1, c:c + 1],
                                            ALU.mult, ALU.add).then_inc(work_done, 1)
                elif kind in "kq":
                    half, kh = item[1], item[2] if kind == "k" else KH
                    parts = ks[:, half, :, BANK * kh:BANK * kh + BANK] if kind == "k" else qs[:, half, :, :]
                    at = half * HALF_TILES + kh
                    wait(dve, split_done, (U + 1) * TILES + (at - 1))
                    b = K if kind == "k" else Q
                    nc.vector.tensor_scalar(full[:, at % 2, :], src, bqk[:, nl, b, half:half + 1], None,
                                            ALU.add).then_inc(work_done, 1)
                    dve.wait_ge(work_done, n + 1)
                    nc.vector.tensor_copy(parts[:, 0, :], full[:, at % 2, :]).then_inc(high_done, 1)
                elif kind == "v":
                    if item[1] == 0:
                        wait(dve, v_placed, (U + 1) * NG)
                    nc.vector.tensor_tensor(vs[:, 2 * item[1]:2 * item[1] + 2, :],
                                            src.rearrange("p (j n) -> p j n", j=2),
                                            bv[:, nl:nl + 1, :].to_broadcast([P, 2, D]),
                                            ALU.add).then_inc(work_done, 1)
                else:
                    empty_o(src, u.before, U, item[1])
                    if item[1] == 1 and u.before == 0:
                        variance(y, 0, u.work(item) + 1, stat_link, (U - 1) * 5, var_ready)

            def empty_o(src, layer, index, o):
                if o == 0:
                    dve.wait_ge(resb_ready, index)
                    if layer == 0:
                        dve.wait_ge(v_placed, index * NG + NG)
                dst = y if layer == 0 else fin
                nc.vector.tensor_tensor(dst[:, 2 * o:2 * o + 2, :], src.rearrange("p (j n) -> p j n", j=2),
                                        resb[:, 2 * o:2 * o + 2, :], ALU.add).then_inc(work_done, 1)

            def variance(t, s, n, link, at, ready):
                if n is not None:
                    dve.wait_ge(work_done, n)
                for qb in range(QB):
                    nc.vector.bn_stats(stats[:, s, qb, :], t[:, qb, :]).then_inc(link, 1)
                dve.wait_ge(link, at + QB)
                settle(dve, "dve")
                for qb in range(QB):
                    last = nc.vector.bn_aggr(mv[:, s, qb, :], stats[:, s, qb, :])
                last.then_inc(link, 1)
                dve.wait_ge(link, at + QB + 1)
                nc.vector.tensor_scalar(var[:, s, :], mv[:, s, :, 1], LN_EPS, None, ALU.add).then_inc(ready, 1)

            def split_max(u, g, n):
                count = u.index * NG + (g or NG)
                dve.wait_ge(work_done, n)
                nc.vector.tensor_tensor(nm[:], negmax[:, 0, :], negmax[:, 1, :], ALU.min).then_inc(max_link, 1)
                dve.wait_ge(max_link, count * 2 + 1)
                nc.vector.tensor_copy(nm_parts[:, 0, :], nm[:]).then_inc(max_link, 1)
                dve.wait_ge(max_link, count * 2 + 2)
                nc.vector.tensor_tensor(nm_parts[:, 1, :], nm[:], nm_parts[:, 0, :],
                                        ALU.subtract).then_inc(max_split, 1)

            def normalize_attn(index, half):
                for p in range(2):
                    dve.wait_ge(o_moved[p], (index * NC + half + 1) * 32)
                nc.vector.reciprocal(rden[:], den[:]).then_inc(attn_link, 1)
                dve.wait_ge(attn_link, index * NC + half + 1)
                nc.vector.tensor_tensor(attn_t[:, half, :], num[:], rden[:], ALU.mult).then_inc(attn_ready, 1)

            for item in prologue.order:
                work(prologue, item)

            dve.wait_ge(wts_in[1], 4 * 16)
            for m in range(4):
                nc.vector.tensor_reduce(absum[:, m:m + 1], wts[:, 1, m, :, :].rearrange("p c n -> p (c n)"),
                                        AX.X, ALU.add, apply_absolute_value=True).then_inc(abs_summed, 1)
            dve.wait_ge(total_ready, 1)
            nc.vector.tensor_scalar(gam[:], po[:, 1, 0:4], 1.0 / (D * D), None, ALU.mult).then_inc(quant_link, 1)
            dve.wait_ge(quant_link, 1)
            for s, sign in ((0, 0.5), (1, -0.5)):
                nc.vector.tensor_scalar(thr[:, s, :], gam[:], QUANT_EPS, sign, ALU.add, ALU.mult
                                        ).then_inc(quant_link, 1)

            def quantize(m):
                at = 3 + 5 * m
                w = wts[:, 1, m, :, :]
                g1 = gam[:, m:m + 1]
                dve.wait_ge(quant_link, at)
                nc.vector.tensor_scalar(tern[:, 0], w, thr[:, 0, m:m + 1], g1, ALU.is_gt, ALU.mult
                                        ).then_inc(quant_link, 1)
                nc.vector.tensor_scalar(tern[:, 1], w, thr[:, 1, m:m + 1], g1, ALU.is_lt, ALU.mult
                                        ).then_inc(quant_link, 1)
                dve.wait_ge(quant_link, at + 2)
                nc.vector.tensor_tensor(tern[:, 0], tern[:, 0], tern[:, 1], ALU.subtract).then_inc(quant_link, 1)
                dve.wait_ge(quant_link, at + 3)
                nc.vector.tensor_tensor(tern[:, 0], tern[:, 0], w, ALU.subtract).then_inc(quant_link, 1)
                dve.wait_ge(quant_link, at + 4)
                nc.vector.tensor_tensor(w, w, tern[:, 0], ALU.add).then_inc(quant_link, 1)

            def unit(u):
                for g in range(NG):
                    for kb in range(KB):
                        for item in u.plan[g, kb]:
                            work(u, item)
                        if g == 0 and kb == 1 and u.after == 1:
                            count = u.index - (B - 1)
                            dve.wait_ge(rows_in, count * 16 + 16)
                            variance(rows, 1, None, rstat_link, count * 5, rvar_ready)
                        if g == 0 and kb == 4 and u.before is not None:
                            normalize_attn(u.index - 1, 1)
                        if g == 2 and kb == 4:
                            normalize_attn(u.index, 0)
                        if kb == 5 and u.before is None:
                            quantize(g)

            run_units(dve, unit)
            normalize_attn(2 * B - 1, 1)
            for o in range(2):
                dve.wait_ge(work_full, W_LAST + o + 1)
                empty_o(pw[:, (W_LAST + o) % 2, :], 1, 2 * B, o)

        @block.gpsimd
        def _(pool):
            def split(index, at):
                half, kh = at // HALF_TILES, at % HALF_TILES
                parts = ks[:, half, :, BANK * kh:BANK * kh + BANK] if kh < KH else qs[:, half, :, :]
                t = full[:, at % 2, :]
                n = index * TILES + at
                pool.wait_ge(high_done, n + 1)
                wait(pool, split_done, n)
                nc.gpsimd.tensor_tensor(rest[:], t, parts[:, 0, :], ALU.subtract).then_inc(split_link, 1)
                pool.wait_ge(split_link, n * 2 + 1)
                settle(pool, "pool")
                nc.gpsimd.tensor_copy(parts[:, 1, :], rest[:]).then_inc(split_link, 1)
                pool.wait_ge(split_link, n * 2 + 2)
                nc.gpsimd.tensor_tensor(parts[:, 2, :], rest[:], parts[:, 1, :], ALU.subtract
                                        ).then_inc(split_done, 1)

            def place_v(g):
                settle(pool, "pool")
                nc.gpsimd.tensor_copy(vx[:, g, :, :, 0:2 * DH:2],
                                      vs[:, :, GH * DH * g:GH * DH * (g + 1)].rearrange(
                                          "p k (h d) -> p k h d", h=GH)).then_inc(v_placed, 1)

            def add_bias(index, layer):
                pool.wait_ge(res_in, index * 16 + 16)
                nc.gpsimd.tensor_tensor(resb[:], res[:], bo[:, layer:layer + 1, :].to_broadcast([P, QB, D]),
                                        ALU.add).then_inc(resb_ready, 1)

            def standardize(dst, src, s, link, at, ready=None):
                nc.gpsimd.tensor_tensor(rstd[:, s, :], var[:, s, :], mhalf[:], ALU.pow).then_inc(link, 1)
                pool.wait_ge(link, at + 1)
                settle(pool, "pool")
                for qb in range(QB):
                    last = nc.gpsimd.tensor_scalar(dst[:, qb, :], src[:, qb, :], mv[:, s, qb, 0:1],
                                                   rstd[:, s, qb:qb + 1], ALU.subtract, ALU.mult)
                last.then_inc(ready or link, 1)

            pool.wait_ge(const_in, N_CONST * 16)
            for at in range(TILES):
                split(0, at)
            pool.wait_ge(consts_set, 1)
            pool.wait_ge(work_done, prologue.work(("v", 3)) + 1)
            for g in range(NG):
                place_v(g)

            def unit(u):
                U = u.index
                if u.before is not None:
                    pool.wait_ge(pv_done, U * (NG * KB))
                    place_v(NG - 1)
                if u.after == 1:
                    pool.wait_ge(rvar_ready, U - (B - 1) + 1)
                    pool.wait_ge(work_done, u.w0)
                    standardize(rows_n, rows, 1, rnorm_link, U - (B - 1), rows_ready)
                if u.after is not None:
                    for at in range(HALF_TILES):
                        split(U + 1, at)
                if u.before is not None:
                    pool.wait_ge(work_done, u.w0)
                    add_bias(U - 1, u.before)
                if u.before == 0:
                    pool.wait_ge(var_ready, U)
                    standardize(y, y, 0, norm_link, (U - 1) * 3)
                    pool.wait_ge(norm_link, (U - 1) * 3 + 2)
                    nc.gpsimd.tensor_tensor(y[:], y[:], ln0[:, 0:1, :].to_broadcast([P, QB, D]), ALU.mult
                                            ).then_inc(norm_link, 1)
                    pool.wait_ge(norm_link, (U - 1) * 3 + 3)
                    nc.gpsimd.tensor_tensor(fin[:], y[:], ln0[:, 1:2, :].to_broadcast([P, QB, D]), ALU.add
                                            ).then_inc(fin_ready, 1)

                if u.after is not None:
                    for at in range(HALF_TILES, TILES):
                        split(U + 1, at)
                    pool.wait_ge(work_done, u.work(("v", 3)) + 1)
                    for g in range(NG - 1):
                        pool.wait_ge(pv_done, U * (NG * KB) + (g + 1) * KB)
                        place_v(g)

            run_units(pool, unit)
            pool.wait_ge(work_done, W_LAST)
            add_bias(2 * B - 1, 1)


def kernel(**inputs):
    import numpy as np
    import concourse.bacc as _bacc
    from concourse import mybir as _mybir
    from concourse.bass_utils import run_bass_kernel_spmd as _run

    i = {k: np.asarray(v) for k, v in inputs.items()}
    perm = np.arange(D).reshape(NC, 2, GH, DH).transpose(0, 1, 3, 2).reshape(-1)
    w0 = i["L0_xattn_W_qkv"]
    b0 = i["L0_xattn_b_qkv"]
    wts = np.stack([
        np.stack([w0[:D][perm].T, w0[D:2 * D][perm].T, w0[2 * D:].T, i["L0_xattn_W_o"].T]),
        np.stack([i["L1_xattn_Wq"][perm].T, i["L1_xattn_Wk"][perm].T, i["L1_xattn_Wv"].T, i["L1_xattn_Wo"].T]),
    ])
    bqk = np.stack([b0[:D][perm], b0[D:2 * D][perm], i["L1_xattn_bq"][perm], i["L1_xattn_bk"][perm]])
    arrays = {
        "x": i["x"],
        "xT": i["x"].transpose(0, 2, 1),
        "ctxT": i["ctx_1024"].transpose(0, 2, 1),
        "wts": wts,
        "bqk": bqk.reshape(4 * NC, P).T,
        "bv": np.stack([b0[2 * D:], i["L1_xattn_bv"]]),
        "bo": np.stack([i["L0_xattn_b_o"], i["L1_xattn_bo"]]),
        "ln0": np.stack([i["L0_xattn_ln_gamma"], i["L0_xattn_ln_beta"]]),
        "ln1": np.stack([i["L1_xattn_ln_gamma"], i["L1_xattn_ln_beta"]]).reshape(2 * NC, P).T,
        "eye": np.eye(P, dtype=np.float32),
    }
    nc = _bacc.Bacc("TRN2", target_bir_lowering=False, num_devices=1)
    feeds, args = {}, {}
    for name, v in arrays.items():
        v = np.ascontiguousarray(v)
        feeds[f"in_{name}"] = v
        args[name] = nc.dram_tensor(f"in_{name}", v.shape, _mybir.dt.from_np(v.dtype), kind="ExternalInput").ap()
    out = nc.dram_tensor("out_0", (B, SQ, D), _mybir.dt.float32, kind="ExternalOutput").ap()
    xattn_two_layers(nc, args, out)
    r = _run(nc, [feeds], core_ids=[0])
    return r.results[0]["out_0"]
```

```python
from contextlib import ExitStack

import concourse.bass as bass
from concourse import mybir

ALU = mybir.AluOpType
ACT = mybir.ActivationFunctionType
AX = mybir.AxisListType
F32 = mybir.dt.float32
BF16 = mybir.dt.bfloat16

P = 128
B, SQ, SK, D, H = 8, 512, 1024, 256, 16
DH = D // H
GH = 4
NG = H // GH
QB = SQ // P
KB = SK // P
NC = D // P
BANK = 512
KH = SK // BANK
K_PART = (0, 1, 2, 0, 1, 0)
Q_PART = (0, 0, 0, 1, 1, 2)
NT = len(K_PART)
ROWS = NT * DH
SROWS = ROWS + 2
LN_EPS = 1e-5
QUANT_EPS = 1e-5
SCALE = float(DH) ** -0.5
HALF_TILES = KH + 1
TILES = NC * HALF_TILES
MAX_AHEAD = 2
MAX_TILES = (5, 5, 4, 4, 4, 4, 4, 2)
WORK_BANKS = 3
Q, K, V, O = range(4)


def v_items(layer):
    n = (2, 2, 2, 2) if layer == 0 else (2, 2, 2, 1, 1)
    return [("v", sum(n[:i]), n[i]) for i in range(len(n))]


def side_items(before, after):
    at = {}
    if after is not None:
        v = v_items(after)
        at.update({(0, 2): [("k", 0, 0)], (0, 3): [("k", 0, 1)], (0, 6): [("q", 0)], (0, 7): [v[0]],
                   (1, 4): [v[1]], (1, 6): [v[2]],
                   (2, 0): [("k", 1, 0)], (2, 2): [("k", 1, 1)], (2, 4): [("q", 1)], (2, 6): v[3:]})
    if after == 1:
        at.update({(0, 5): [("xnT", c) for c in range(NC)]})
    if before is not None:
        at.update({(1, 1): [("o", 0)], (1, 2): [("o", 1)]})
    return at


def scalar_empties(item):
    return item[0] in "kq"


def tile_of(item):
    return item[1] * HALF_TILES + (item[2] if item[0] == "k" else KH)


def max_items(g):
    return [("max", g, h, qb, kh) for h in range(GH) for qb in range(QB) for kh in range(KH)]


class Unit:

    def __init__(self, index, layer, batch, w0, v0, bank, before, after):
        self.index, self.layer, self.batch = index, layer, batch
        self.w0, self.v0, self.bank, self.before, self.after = w0, v0, bank, before, after
        self.plan = {}
        side = side_items(before, after)
        for g in range(NG):
            ahead = (g + MAX_AHEAD) % NG
            todo = max_items(ahead) if g + MAX_AHEAD < NG or after is not None else []
            turn = [("maxT", ahead)] if todo else []
            for kb, n in enumerate(MAX_TILES):
                self.plan[g, kb], todo = todo[:n] + side.get((g, kb), []), todo[n:]
            self.plan[g, KB - 1] += turn
        self.number_items([item for at in sorted(self.plan) for item in self.plan[at]])

    def number_items(self, order):
        self.order = order
        self.number = {item: n for n, item in enumerate(order)}
        mine = [item for item in order if not scalar_empties(item)]
        self.vector_number = {item: n for n, item in enumerate(mine)}

    def filled(self, item):
        return self.w0 + self.number[item] + 1

    def emptied(self, item):
        return self.v0 + self.vector_number[item] + 1

    def ahead(self, g):
        return self.index * NG + (g if g >= MAX_AHEAD else g + NG)

    def slot(self, item):
        return (self.bank + self.number[item]) % WORK_BANKS


class Prologue(Unit):

    def __init__(self):
        self.index, self.layer, self.batch, self.w0, self.v0, self.bank = -1, 0, -1, 0, 0, 0
        self.before, self.after = None, 0
        self.number_items([("k", 0, 0), ("k", 0, 1), ("q", 0)] + v_items(0)
                      + [("k", 1, 0), ("k", 1, 1), ("q", 1)]
                      + [i for g in range(MAX_AHEAD) for i in max_items(g) + [("maxT", g)]])


def plan_units():
    prologue = Prologue()
    w, v = len(prologue.order), len(prologue.vector_number)
    entries = []
    for layer in range(2):
        for batch in (0, 1, B - 1):
            before = None if layer == 0 and batch == 0 else (0 if batch == 0 else layer)
            after = (1 if layer == 0 else None) if batch == B - 1 else layer
            unit = Unit(0, layer, batch, 0, 0, 0, before, after)
            n, nv = len(unit.order), len(unit.vector_number)
            entries.append((layer, batch, w, n, v, nv, before, after))
            w += n * (B - 2 if batch == 1 else 1)
            v += nv * (B - 2 if batch == 1 else 1)
            assert batch != 1 or n % WORK_BANKS == 0
    return prologue, entries


def xattn_two_layers(nc, a, out):
    x_in = {0: a["x"], 1: nc.dram_tensor("layer0_out", (B, SQ, D), F32, kind="Internal").ap()}
    x_out = {0: x_in[1], 1: out}
    prologue, entries = plan_units()

    def run_units(eng, body):
        for layer, batch, w, n, v, nv, before, after in entries:
            if batch == 1:
                with eng.Fori(1, B - 1) as i:
                    body(Unit(i + layer * B if layer else i, layer, i, (i - 1) * n + w, (i - 1) * nv + v,
                              w % WORK_BANKS, before, after))
            else:
                body(Unit(layer * B + batch, layer, batch, w, v, w % WORK_BANKS, before, after))

    with ExitStack() as ctx:
        def sb(name, shape, dt=F32):
            return ctx.enter_context(nc.sbuf_tensor(name, shape, dt))

        def sem(name):
            return ctx.enter_context(nc.semaphore(name))

        k6 = sb("k6", [P, H, SK], BF16)
        q6 = sb("q6", [P, H, SQ], BF16)
        vx = sb("vx", [P, NG, KB, GH, 2 * DH])
        probs = sb("probs", [P, 2, GH, SQ])
        ctx_t = sb("ctx_t", [P, NC, SK])
        x_t = sb("x_t", [P, NC, SQ])
        full = sb("full", [P, 2, BANK])
        rest = sb("rest", [P, BANK])
        ks = sb("ks", [P, NC, 3, SK], BF16)
        qs = sb("qs", [P, NC, 3, SQ], BF16)
        vs = sb("vs", [P, KB, D])
        rows = sb("rows", [P, QB, D])
        rows_n = sb("rows_n", [P, QB, D])
        o_raw = sb("o_raw", [P, 2, SQ])
        num = sb("num", [P, SQ])
        den = sb("den", [P, SQ])
        rden = sb("rden", [P, SQ])
        attn_t = sb("attn_t", [P, NC, SQ])
        res = sb("res", [P, QB, D])
        resb = sb("resb", [P, QB, D])
        y = sb("y", [P, QB, D])
        fin = sb("fin", [P, QB, D])
        negmax = sb("negmax", [P, KH, GH * QB])
        nm = sb("nm", [P, GH * QB])
        nm_parts = sb("nm_parts", [P, 2, GH * QB], BF16)
        nm_t = sb("nm_t", [2 * GH * QB, P], BF16)
        stats = sb("stats", [P, 2, QB, 6])
        mv = sb("mv", [P, 2, QB, 2])
        var = sb("var", [P, 2, QB])
        rstd = sb("rstd", [P, 2, QB])
        wts = sb("wts", [P, 2, 4, NC, D])
        absum = sb("absum", [P, 4])
        gam = sb("gam", [P, 4])
        thr = sb("thr", [P, 2, 4])
        tern = sb("tern", [P, 2, NC, D])
        ones = sb("ones", [P, P])
        eye = sb("eye", [P, P])
        eyeb = sb("eyeb", [P, P], BF16)
        mhalf = sb("mhalf", [P, QB])
        bqk = sb("bqk", [P, 2, 2, NC])
        bv = sb("bv", [P, 2, D])
        bo = sb("bo", [P, 2, D])
        ln0 = sb("ln0", [P, 2, D])
        ln1 = sb("ln1", [P, 2, NC])

        ps = ctx.enter_context(nc.psum_tensor("ps", [P, 2, 2 * BANK], F32))
        pw = ctx.enter_context(nc.psum_tensor("pw", [P, WORK_BANKS, BANK], F32))
        po = ctx.enter_context(nc.psum_tensor("po", [P, BANK], F32))

        const_in = sem("const_in")
        wts_in = [sem(f"wts_in{l}") for l in range(2)]
        ctx_in = sem("ctx_in")
        x_t_in = sem("x_t_in")
        rows_in = sem("rows_in")
        res_in = sem("res_in")
        restacked = [sem(f"restacked{g}") for g in range(NG)]
        max_placed = sem("max_placed")
        o_moved = [sem(f"o_moved{p}") for p in range(2)]
        stored = sem("stored")
        consts_set = sem("consts_set")
        ones_set = sem("ones_set")
        abs_summed = sem("abs_summed")
        total_ready = sem("total_ready")
        quant_link = sem("quant_link")
        work_full = sem("work_full")
        work_done = sem("work_done")
        scores_full = sem("scores_full")
        probs_ready = sem("probs_ready")
        pv_done = sem("pv_done")
        o_copied = sem("o_copied")
        tile_full = sem("tile_full")
        split_link = sem("split_link")
        split_done = sem("split_done")
        v_placed = sem("v_placed")
        max_link = sem("max_link")
        max_split = sem("max_split")
        attn_link = sem("attn_link")
        attn_ready = sem("attn_ready")
        resb_ready = sem("resb_ready")
        stat_link = sem("stat_link")
        var_ready = sem("var_ready")
        norm_link = sem("norm_link")
        fin_ready = sem("fin_ready")
        rstat_link = sem("rstat_link")
        rvar_ready = sem("rvar_ready")
        rnorm_link = sem("rnorm_link")
        rows_ready = sem("rows_ready")

        settled = {e: sem(f"settled_{e}") for e in ("sp", "dve", "pool")}

        def settle(eng, name):
            eng.sem_inc(settled[name], 1)

        def wait(eng, sem, count):
            if not isinstance(count, int) or count > 0:
                eng.wait_ge(sem, count)
                if eng is nc.sync and not isinstance(count, int):
                    settle(eng, "sp")

        block = ctx.enter_context(nc.Block())
        N_CONST = 9
        W_LAST = entries[-1][2] + entries[-1][3]
        V_LAST = entries[-1][4] + entries[-1][5]

        def split_parts(half, at):
            return ks[:, half, :, BANK * at:BANK * at + BANK] if at < KH else qs[:, half, :, :]

        def rows_of(dram, batch):
            return dram[batch].rearrange("(t p) d -> p t d", p=P)

        @block.sync
        def _(sp):
            def load_inputs(layer, batch):
                sp.dma_start(ctx_t[:], a["ctxT"][batch].rearrange("(c p) n -> p c n", p=P)).then_inc(ctx_in, 16)
                if layer == 0:
                    sp.dma_start(x_t[:], a["xT"][batch].rearrange("(c p) n -> p c n", p=P)).then_inc(x_t_in, 16)

            def restack(index, g):
                half, lane = g // 2, 64 * (g % 2)
                wait(sp, split_done, index * TILES + (half + 1) * HALF_TILES)
                for t in range(NT):
                    sp.dma_start(k6[DH * t:DH * t + DH, GH * g:GH * g + GH, :],
                                 ks[lane:lane + 64, half, K_PART[t], :]).then_inc(restacked[g], 16)
                    sp.dma_start(q6[DH * t:DH * t + DH, GH * g:GH * g + GH, :],
                                 qs[lane:lane + 64, half, Q_PART[t], :]).then_inc(restacked[g], 16)

            def place_max(u, g):
                wait(sp, work_done, u.emptied(("maxT", g)))
                sp.dma_start(q6[ROWS:SROWS, GH * g:GH * g + GH, :], nm_t[:, :]).then_inc(max_placed, 16)

            def move_o(index, g):
                wait(sp, o_copied, index * NG + g + 1)
                wait(sp, attn_ready, index * NC + g // 2)
                lane = 64 * (g % 2)
                for c, t in ((0, num), (1, den)):
                    sp.dma_start(t[lane:lane + 64, :], o_raw[c:P:2, g % 2, :]).then_inc(o_moved[g % 2], 16)

            def load_residual(index, layer, batch):
                if layer == 1:
                    wait(sp, stored, batch * 16 + 16)
                sp.dma_start(res[:], rows_of(x_in[layer], batch)).then_inc(res_in, 16)

            load_inputs(0, 0)
            sp.dma_start(bqk[:].rearrange("p l k c -> p (l k c)"), a["bqk"]).then_inc(const_in, 16)
            sp.dma_start(eye[:], a["eye"]).then_inc(const_in, 16)
            for l in range(2):
                sp.dma_start(bv[:, l, :], a["bv"][l:l + 1, :].to_broadcast([P, D])).then_inc(const_in, 16)
                sp.dma_start(bo[:, l, :], a["bo"][l:l + 1, :].to_broadcast([P, D])).then_inc(const_in, 16)
                sp.dma_start(ln0[:, l, :], a["ln0"][l:l + 1, :].to_broadcast([P, D])).then_inc(const_in, 16)
            sp.dma_start(ln1[:].rearrange("p k c -> p (k c)"), a["ln1"]).then_inc(const_in, 16)
            for g in range(NG):
                restack(0, g)
            for g in range(MAX_AHEAD):
                place_max(prologue, g)

            def unit(u):
                U = u.index
                wait(sp, work_done, u.v0)
                if u.after is not None:
                    next_batch = 0 if u.after != u.layer else u.batch + 1
                    load_inputs(u.after, next_batch)
                    if u.after == 1:
                        if u.layer == 1:
                            wait(sp, rows_ready, U - (B - 1))
                        wait(sp, stored, next_batch * 16 + 16)
                        sp.dma_start(rows[:], rows_of(x_in[1], next_batch)).then_inc(rows_in, 16)
                if u.before is not None:
                    last_batch = B - 1 if u.before != u.layer else u.batch - 1
                    move_o(U - 1, NG - 1)
                    wait(sp, scores_full, U * (NG * KB * 2))
                    restack(U, NG - 1)
                    load_residual(U - 1, u.before, last_batch)
                for g in range(NG):
                    if g > 0:
                        move_o(U, g - 1)
                        if u.after is not None:
                            wait(sp, scores_full, U * (NG * KB * 2) + g * KB * 2)
                            restack(U + 1, g - 1)
                    if g + MAX_AHEAD < NG or u.after is not None:
                        place_max(u, (g + MAX_AHEAD) % NG)
                if u.before is not None:
                    if u.before == 0:
                        wait(sp, fin_ready, U)
                    else:
                        wait(sp, work_done, u.emptied(("o", 1)))
                    sp.dma_start(rows_of(x_out[u.before], last_batch), fin[:]).then_inc(stored, 16)
                    wait(sp, stored, U * 16)

            run_units(sp, unit)
            move_o(2 * B - 1, NG - 1)
            wait(sp, work_done, V_LAST)
            load_residual(2 * B - 1, 1, B - 1)
            wait(sp, work_done, V_LAST + 2)
            sp.dma_start(rows_of(out, B - 1), fin[:]).then_inc(stored, 16)
            wait(sp, stored, 2 * B * 16)

        @block.tensor
        def _(pe):
            def start_work(u, item):
                n = u.number[item] - WORK_BANKS
                if n < 0:
                    wait(pe, work_done, u.v0 + (n + 1))
                elif scalar_empties(u.order[n]):
                    pe.wait_ge(tile_full, (u.index + 1) * TILES + tile_of(u.order[n]) + 1)
                else:
                    pe.wait_ge(work_done, u.emptied(u.order[n]))
                return pw[:, u.slot(item), :]

            def o_proj(dst, layer, o):
                for j in range(2):
                    qb = 2 * o + j
                    for c in range(NC):
                        mm = nc.tensor.matmul(dst[:, D * j:D * j + D], attn_t[:, c, P * qb:P * qb + P],
                                              wts[:, layer, O, c, :], start=(c == 0), stop=(c == NC - 1))
                return mm

            def work(u, item):
                dst = start_work(u, item)
                kind, nl, U = item[0], u.after, u.index
                if kind == "max":
                    _, g, h, qb, kh = item
                    if (h, qb, kh) == (0, 0, 0):
                        pe.wait_ge(restacked[g], (U + (g < MAX_AHEAD)) * (2 * NT * 16) + 2 * NT * 16)
                    s = GH * g + h
                    mm = nc.tensor.matmul(dst, q6[0:ROWS, s, P * qb:P * qb + P],
                                          k6[0:ROWS, s, BANK * kh:BANK * kh + BANK], start=True, stop=True)
                elif kind == "maxT":
                    pe.wait_ge(max_split, u.ahead(item[1]) + 1)
                    mm = nc.tensor.transpose(dst.bitcast(BF16)[0:2 * GH * QB, 0:P],
                                             nm_parts[:].rearrange("p k n -> p (k n)"), eyeb[:])
                elif kind == "xnT":
                    pe.wait_ge(rows_ready, U - (B - 1) + 1)
                    for qb in range(QB):
                        mm = nc.tensor.transpose(dst[:, P * qb:P * qb + P],
                                                 rows_n[:, qb, P * item[1]:P * item[1] + P], eye[:])
                elif kind == "k":
                    _, half, kh = item
                    if (half, kh) == (0, 0):
                        pe.wait_ge(ctx_in, U * 16 + 32)
                    for c in range(NC):
                        mm = nc.tensor.matmul(dst, wts[:, nl, K, c, P * half:P * half + P],
                                              ctx_t[:, c, BANK * kh:BANK * kh + BANK],
                                              start=(c == 0), stop=(c == NC - 1))
                elif kind == "q":
                    half = item[1]
                    if half == 0:
                        if nl == 0:
                            pe.wait_ge(x_t_in, U * 16 + 32)
                        else:
                            pe.wait_ge(work_done, u.emptied(("xnT", NC - 1)))
                    for c in range(NC):
                        mm = nc.tensor.matmul(dst, wts[:, nl, Q, c, P * half:P * half + P], x_t[:, c, :],
                                              start=(c == 0), stop=(c == NC - 1))
                elif kind == "v":
                    for j in range(item[2]):
                        kb = item[1] + j
                        for c in range(NC):
                            mm = nc.tensor.matmul(dst[:, D * j:D * j + D], ctx_t[:, c, P * kb:P * kb + P],
                                                  wts[:, nl, V, c, :], start=(c == 0), stop=(c == NC - 1))
                else:
                    if item[1] == 0:
                        pe.wait_ge(attn_ready, U * NC)
                    mm = o_proj(dst, u.before, item[1])
                mm.then_inc(work_full, 1)

            def scores(u, g, kb, p):
                step = u.index * (NG * KB) + (g * KB + kb)
                if kb == 0 and p == 0:
                    pe.wait_ge(max_placed, (u.index * NG + g + 1) * 16)
                wait(pe, probs_ready, step * 2 + (p - 1))
                for j in range(2):
                    s = GH * g + 2 * p + j
                    mm = nc.tensor.matmul(ps[:, p, BANK * j:BANK * j + BANK],
                                          k6[0:SROWS, s, P * kb:P * kb + P], q6[0:SROWS, s, :],
                                          start=True, stop=True)
                mm.then_inc(scores_full, 1)

            def values(index, g, kb):
                if kb == 0:
                    pe.wait_ge(v_placed, index * NG + g + 1)
                    wait(pe, o_copied, index * NG + g)
                pe.wait_ge(probs_ready, index * (NG * KB * 2) + (g * KB + kb + 1) * 2)
                for h in range(GH):
                    mm = nc.tensor.matmul(po[32 * h:32 * h + 32, :], vx[:, g, kb, h, :],
                                          probs[:, kb % 2, h, :], start=(kb == 0), stop=(kb == KB - 1))
                mm.then_inc(pv_done, 1)

            pe.wait_ge(const_in, N_CONST * 16)
            pe.wait_ge(wts_in[0], 4 * 16)
            pe.wait_ge(consts_set, 1)
            for item in prologue.order:
                work(prologue, item)
            pe.wait_ge(abs_summed, 4)
            nc.tensor.matmul(po[:, 0:4], ones[:], absum[:], start=True, stop=True).then_inc(total_ready, 1)

            def unit(u):
                for g in range(NG):
                    for kb in range(KB):
                        items = u.plan[g, kb]
                        for item in items[0:1]:
                            work(u, item)
                        scores(u, g, kb, 0)
                        for item in items[1:2]:
                            work(u, item)
                        scores(u, g, kb, 1)
                        for item in items[2:3]:
                            work(u, item)
                        if kb > 0:
                            values(u.index, g, kb - 1)
                        elif g > 0:
                            values(u.index, g - 1, KB - 1)
                        elif u.before is not None:
                            values(u.index - 1, NG - 1, KB - 1)
                        for item in items[3:]:
                            work(u, item)

            run_units(pe, unit)
            values(2 * B - 1, NG - 1, KB - 1)
            pe.wait_ge(attn_ready, 2 * B * NC)
            for o in range(2):
                pe.wait_ge(work_done, V_LAST + o + 1 - WORK_BANKS)
                o_proj(pw[:, (W_LAST + o) % WORK_BANKS, :], 1, o).then_inc(work_full, 1)

        @block.scalar
        def _(act):
            for l in range(2):
                for m in range(4):
                    act.dma_start(wts[:, l, m, :, :], a["wts"][l, m].rearrange("(c p) n -> p c n", p=P)
                                  ).then_inc(wts_in[l], 16)

            def copy_o(index, g):
                act.wait_ge(pv_done, index * (NG * KB) + (g + 1) * KB)
                wait(act, o_moved[g % 2], (index * NC + g // 2) * 32)
                nc.scalar.copy(o_raw[:, g % 2, :], po[:]).then_inc(o_copied, 1)

            def project(u, item):
                half, at = item[1], tile_of(item)
                n = (u.index + 1) * TILES + at
                parts, src = split_parts(half, at % HALF_TILES), pw[:, u.slot(item), :]
                bias = bqk[:, u.after, K if item[0] == "k" else Q, half:half + 1]
                act.wait_ge(work_full, u.filled(item))
                nc.scalar.activation(parts[:, 0, :], src, ACT.Identity, bias=bias)
                wait(act, split_done, n - 1)
                nc.scalar.activation(full[:, at % 2, :], src, ACT.Identity, bias=bias).then_inc(tile_full, 1)

            act.wait_ge(const_in, N_CONST * 16)
            for item in prologue.order:
                if scalar_empties(item):
                    project(prologue, item)

            def unit(u):
                for g in range(NG):
                    for kb in range(KB):
                        step = u.index * (NG * KB) + (g * KB + kb)
                        wait(act, pv_done, step - 1)
                        for p in range(2):
                            act.wait_ge(scores_full, step * 2 + (p + 1))
                            nc.scalar.activation(probs[:, kb % 2, 2 * p:2 * p + 2, :].rearrange("p h n -> p (h n)"),
                                                 ps[:, p, :], ACT.Exp, scale=SCALE).then_inc(probs_ready, 1)
                        if kb == 0 and g > 0:
                            copy_o(u.index, g - 1)
                        elif kb == 0 and u.before is not None:
                            copy_o(u.index - 1, NG - 1)
                        for item in u.plan[g, kb]:
                            if scalar_empties(item):
                                project(u, item)

            run_units(act, unit)
            copy_o(2 * B - 1, NG - 1)

        @block.vector
        def _(dve):
            nc.vector.memset(ones[:], 1.0)
            nc.vector.memset(mhalf[:], -0.5)
            nc.vector.memset(k6[ROWS:SROWS, :, :], 1.0)
            nc.vector.memset(vx[:, :, :, :, 1:2 * DH:2], 1.0)
            dve.wait_ge(const_in, N_CONST * 16)
            nc.vector.tensor_copy(eyeb[:], eye[:]).then_inc(consts_set, 1)

            def work(u, item):
                if scalar_empties(item):
                    return
                src = pw[:, u.slot(item), :]
                kind, nl, U, done = item[0], u.after, u.index, u.emptied(item)
                dve.wait_ge(work_full, u.filled(item))
                if kind == "max":
                    _, g, h, qb, kh = item
                    nc.vector.tensor_reduce(negmax[:, kh, QB * h + qb:QB * h + qb + 1], src, AX.X, ALU.max,
                                            negate=True).then_inc(work_done, 1)
                    if (h, qb, kh) == (GH - 1, QB - 1, KH - 1):
                        split_max(u, g, done)
                elif kind == "maxT":
                    wait(dve, max_placed, u.ahead(item[1]) * 16)
                    nc.vector.tensor_copy(nm_t[:], src.bitcast(BF16)[0:2 * GH * QB, 0:P]).then_inc(work_done, 1)
                elif kind == "xnT":
                    c = item[1]
                    nc.vector.tensor_scalar(x_t[:, c, :], src, ln1[:, 0, c:c + 1], ln1[:, 1, c:c + 1],
                                            ALU.mult, ALU.add).then_inc(work_done, 1)
                elif kind == "v":
                    if item[1] == 0:
                        wait(dve, v_placed, (U + 1) * NG)
                    n = item[2]
                    nc.vector.tensor_tensor(vs[:, item[1]:item[1] + n, :],
                                            src[:, 0:D * n].rearrange("p (j n) -> p j n", j=n),
                                            bv[:, nl:nl + 1, :].to_broadcast([P, n, D]),
                                            ALU.add).then_inc(work_done, 1)
                else:
                    empty_o(src, u.before, U, item[1])
                    if item[1] == 1 and u.before == 0:
                        variance(y, 0, done, stat_link, (U - 1) * 5, var_ready)

            def empty_o(src, layer, index, o):
                if o == 0:
                    dve.wait_ge(resb_ready, index)
                    if layer == 0:
                        dve.wait_ge(v_placed, index * NG + NG)
                dst = y if layer == 0 else fin
                nc.vector.tensor_tensor(dst[:, 2 * o:2 * o + 2, :], src.rearrange("p (j n) -> p j n", j=2),
                                        resb[:, 2 * o:2 * o + 2, :], ALU.add).then_inc(work_done, 1)

            def variance(t, s, n, link, at, ready):
                if n is not None:
                    dve.wait_ge(work_done, n)
                for qb in range(QB):
                    nc.vector.bn_stats(stats[:, s, qb, :], t[:, qb, :]).then_inc(link, 1)
                dve.wait_ge(link, at + QB)
                settle(dve, "dve")
                for qb in range(QB):
                    last = nc.vector.bn_aggr(mv[:, s, qb, :], stats[:, s, qb, :])
                last.then_inc(link, 1)
                dve.wait_ge(link, at + QB + 1)
                nc.vector.tensor_scalar(var[:, s, :], mv[:, s, :, 1], LN_EPS, None, ALU.add).then_inc(ready, 1)

            def split_max(u, g, n):
                count = u.ahead(g)
                dve.wait_ge(work_done, n)
                nc.vector.tensor_tensor(nm[:], negmax[:, 0, :], negmax[:, 1, :], ALU.min).then_inc(max_link, 1)
                dve.wait_ge(max_link, count * 2 + 1)
                nc.vector.tensor_copy(nm_parts[:, 0, :], nm[:]).then_inc(max_link, 1)
                dve.wait_ge(max_link, count * 2 + 2)
                nc.vector.tensor_tensor(nm_parts[:, 1, :], nm[:], nm_parts[:, 0, :],
                                        ALU.subtract).then_inc(max_split, 1)

            def normalize_attn(index, half):
                for p in range(2):
                    dve.wait_ge(o_moved[p], (index * NC + half + 1) * 32)
                nc.vector.reciprocal(rden[:], den[:]).then_inc(attn_link, 1)
                dve.wait_ge(attn_link, index * NC + half + 1)
                nc.vector.tensor_tensor(attn_t[:, half, :], num[:], rden[:], ALU.mult).then_inc(attn_ready, 1)

            for item in prologue.order:
                work(prologue, item)

            dve.wait_ge(wts_in[1], 4 * 16)
            for m in range(4):
                nc.vector.tensor_reduce(absum[:, m:m + 1], wts[:, 1, m, :, :].rearrange("p c n -> p (c n)"),
                                        AX.X, ALU.add, apply_absolute_value=True).then_inc(abs_summed, 1)
            dve.wait_ge(total_ready, 1)
            nc.vector.tensor_scalar(gam[:], po[:, 0:4], 1.0 / (D * D), None, ALU.mult).then_inc(quant_link, 1)
            dve.wait_ge(quant_link, 1)
            for s, sign in ((0, 0.5), (1, -0.5)):
                nc.vector.tensor_scalar(thr[:, s, :], gam[:], QUANT_EPS, sign, ALU.add, ALU.mult
                                        ).then_inc(quant_link, 1)

            def quantize(m):
                at = 3 + 5 * m
                w = wts[:, 1, m, :, :]
                g1 = gam[:, m:m + 1]
                dve.wait_ge(quant_link, at)
                nc.vector.tensor_scalar(tern[:, 0], w, thr[:, 0, m:m + 1], g1, ALU.is_gt, ALU.mult
                                        ).then_inc(quant_link, 1)
                nc.vector.tensor_scalar(tern[:, 1], w, thr[:, 1, m:m + 1], g1, ALU.is_lt, ALU.mult
                                        ).then_inc(quant_link, 1)
                dve.wait_ge(quant_link, at + 2)
                nc.vector.tensor_tensor(tern[:, 0], tern[:, 0], tern[:, 1], ALU.subtract).then_inc(quant_link, 1)
                dve.wait_ge(quant_link, at + 3)
                nc.vector.tensor_tensor(tern[:, 0], tern[:, 0], w, ALU.subtract).then_inc(quant_link, 1)
                dve.wait_ge(quant_link, at + 4)
                nc.vector.tensor_tensor(w, w, tern[:, 0], ALU.add).then_inc(quant_link, 1)

            def unit(u):
                for g in range(NG):
                    for kb in range(KB):
                        for item in u.plan[g, kb]:
                            work(u, item)
                        if g == 0 and kb == 1 and u.after == 1:
                            count = u.index - (B - 1)
                            dve.wait_ge(rows_in, count * 16 + 16)
                            variance(rows, 1, None, rstat_link, count * 5, rvar_ready)
                        if g == 0 and kb == 4 and u.before is not None:
                            normalize_attn(u.index - 1, 1)
                        if g == 2 and kb == 4:
                            normalize_attn(u.index, 0)
                        if kb == 5 and u.before is None:
                            quantize(g)

            run_units(dve, unit)
            normalize_attn(2 * B - 1, 1)
            for o in range(2):
                dve.wait_ge(work_full, W_LAST + o + 1)
                empty_o(pw[:, (W_LAST + o) % WORK_BANKS, :], 1, 2 * B, o)

        @block.gpsimd
        def _(pool):
            def split(index, at):
                parts = split_parts(at // HALF_TILES, at % HALF_TILES)
                t = full[:, at % 2, :]
                n = index * TILES + at
                pool.wait_ge(tile_full, n + 1)
                wait(pool, split_done, n)
                nc.gpsimd.tensor_tensor(rest[:], t, parts[:, 0, :], ALU.subtract).then_inc(split_link, 1)
                pool.wait_ge(split_link, n * 2 + 1)
                settle(pool, "pool")
                nc.gpsimd.tensor_copy(parts[:, 1, :], rest[:]).then_inc(split_link, 1)
                pool.wait_ge(split_link, n * 2 + 2)
                nc.gpsimd.tensor_tensor(parts[:, 2, :], rest[:], parts[:, 1, :], ALU.subtract
                                        ).then_inc(split_done, 1)

            def place_v(g):
                settle(pool, "pool")
                nc.gpsimd.tensor_copy(vx[:, g, :, :, 0:2 * DH:2],
                                      vs[:, :, GH * DH * g:GH * DH * (g + 1)].rearrange(
                                          "p k (h d) -> p k h d", h=GH)).then_inc(v_placed, 1)

            def add_bias(index, layer):
                pool.wait_ge(res_in, index * 16 + 16)
                nc.gpsimd.tensor_tensor(resb[:], res[:], bo[:, layer:layer + 1, :].to_broadcast([P, QB, D]),
                                        ALU.add).then_inc(resb_ready, 1)

            def standardize(dst, src, s, link, at, ready=None):
                nc.gpsimd.tensor_tensor(rstd[:, s, :], var[:, s, :], mhalf[:], ALU.pow).then_inc(link, 1)
                pool.wait_ge(link, at + 1)
                settle(pool, "pool")
                for qb in range(QB):
                    last = nc.gpsimd.tensor_scalar(dst[:, qb, :], src[:, qb, :], mv[:, s, qb, 0:1],
                                                   rstd[:, s, qb:qb + 1], ALU.subtract, ALU.mult)
                last.then_inc(ready or link, 1)

            pool.wait_ge(const_in, N_CONST * 16)
            for at in range(TILES):
                split(0, at)
            pool.wait_ge(consts_set, 1)
            pool.wait_ge(work_done, prologue.emptied(v_items(0)[-1]))
            for g in range(NG):
                place_v(g)

            def unit(u):
                U = u.index
                if u.before is not None:
                    pool.wait_ge(pv_done, U * (NG * KB))
                    place_v(NG - 1)
                if u.after == 1:
                    pool.wait_ge(rvar_ready, U - (B - 1) + 1)
                    pool.wait_ge(work_done, u.v0)
                    standardize(rows_n, rows, 1, rnorm_link, U - (B - 1), rows_ready)
                if u.after is not None:
                    for at in range(HALF_TILES):
                        split(U + 1, at)
                if u.before is not None:
                    pool.wait_ge(work_done, u.v0)
                    add_bias(U - 1, u.before)
                if u.before == 0:
                    pool.wait_ge(var_ready, U)
                    standardize(y, y, 0, norm_link, (U - 1) * 3)
                    pool.wait_ge(norm_link, (U - 1) * 3 + 2)
                    nc.gpsimd.tensor_tensor(y[:], y[:], ln0[:, 0:1, :].to_broadcast([P, QB, D]), ALU.mult
                                            ).then_inc(norm_link, 1)
                    pool.wait_ge(norm_link, (U - 1) * 3 + 3)
                    nc.gpsimd.tensor_tensor(fin[:], y[:], ln0[:, 1:2, :].to_broadcast([P, QB, D]), ALU.add
                                            ).then_inc(fin_ready, 1)

                if u.after is not None:
                    for at in range(HALF_TILES, TILES):
                        split(U + 1, at)
                    pool.wait_ge(work_done, u.emptied(v_items(u.after)[-1]))
                    for g in range(NG - 1):
                        pool.wait_ge(pv_done, U * (NG * KB) + (g + 1) * KB)
                        place_v(g)

            run_units(pool, unit)
            pool.wait_ge(work_done, V_LAST)
            add_bias(2 * B - 1, 1)


def kernel(**inputs):
    import numpy as np
    import concourse.bacc as _bacc
    from concourse import mybir as _mybir
    from concourse.bass_utils import run_bass_kernel_spmd as _run

    i = {k: np.asarray(v) for k, v in inputs.items()}
    perm = np.arange(D).reshape(NC, 2, GH, DH).transpose(0, 1, 3, 2).reshape(-1)
    w0 = i["L0_xattn_W_qkv"]
    b0 = i["L0_xattn_b_qkv"]
    wts = np.stack([
        np.stack([w0[:D][perm].T, w0[D:2 * D][perm].T, w0[2 * D:].T, i["L0_xattn_W_o"].T]),
        np.stack([i["L1_xattn_Wq"][perm].T, i["L1_xattn_Wk"][perm].T, i["L1_xattn_Wv"].T, i["L1_xattn_Wo"].T]),
    ])
    bqk = np.stack([b0[:D][perm], b0[D:2 * D][perm], i["L1_xattn_bq"][perm], i["L1_xattn_bk"][perm]])
    arrays = {
        "x": i["x"],
        "xT": i["x"].transpose(0, 2, 1),
        "ctxT": i["ctx_1024"].transpose(0, 2, 1),
        "wts": wts,
        "bqk": bqk.reshape(4 * NC, P).T,
        "bv": np.stack([b0[2 * D:], i["L1_xattn_bv"]]),
        "bo": np.stack([i["L0_xattn_b_o"], i["L1_xattn_bo"]]),
        "ln0": np.stack([i["L0_xattn_ln_gamma"], i["L0_xattn_ln_beta"]]),
        "ln1": np.stack([i["L1_xattn_ln_gamma"], i["L1_xattn_ln_beta"]]).reshape(2 * NC, P).T,
        "eye": np.eye(P, dtype=np.float32),
    }
    nc = _bacc.Bacc("TRN2", target_bir_lowering=False, num_devices=1)
    feeds, args = {}, {}
    for name, v in arrays.items():
        v = np.ascontiguousarray(v)
        feeds[f"in_{name}"] = v
        args[name] = nc.dram_tensor(f"in_{name}", v.shape, _mybir.dt.from_np(v.dtype), kind="ExternalInput").ap()
    out = nc.dram_tensor("out_0", (B, SQ, D), _mybir.dt.float32, kind="ExternalOutput").ap()
    xattn_two_layers(nc, args, out)
    r = _run(nc, [feeds], core_ids=[0])
    return r.results[0]["out_0"]
```

```python
from contextlib import ExitStack

import concourse.bass as bass
from concourse import mybir

ALU = mybir.AluOpType
ACT = mybir.ActivationFunctionType
AX = mybir.AxisListType
F32 = mybir.dt.float32
BF16 = mybir.dt.bfloat16
F32R = mybir.dt.float32r

P = 128
B, SQ, SK, D, H = 8, 512, 1024, 256, 16
DH = D // H
GH = 4
NG = H // GH
QB = SQ // P
KB = SK // P
NC = D // P
BANK = 512
KH = SK // BANK
K_PART = (0, 1, 2, 0, 1, 0)
Q_PART = (0, 0, 0, 1, 1, 2)
NT = len(K_PART)
ROWS = NT * DH
SROWS = ROWS + 2
LN_EPS = 1e-5
QUANT_EPS = 1e-5
SCALE = float(DH) ** -0.5
HALF_TILES = KH + 1
TILES = NC * HALF_TILES
MAX_AHEAD = 2
MAX_TILES = GH * QB * KH // KB
WORK_BANKS = 3
Q, K, V, O = range(4)


def v_items(layer):
    n = (2, 2, 2, 2) if layer == 0 else (2, 2, 2, 1, 1)
    return [("v", sum(n[:i]), n[i]) for i in range(len(n))]


def side_items(before, after):
    at = {}
    if after is not None:
        v = v_items(after)
        at.update({(0, 5): [("k", 0, 0)], (0, 6): [("k", 0, 1)], (1, 3): [("q", 0)],
                   (1, 4): [v[0]], (1, 5): [v[1]], (1, 7): [v[2]],
                   (2, 0): [("k", 1, 0)], (2, 2): [("k", 1, 1)], (2, 5): [("q", 1)], (2, 7): v[3:]})
    if after == 1:
        at.update({(1, 0): [("xnT", c) for c in range(NC)]})
    if before is not None:
        at.update({(1, 1): [("o", 0)], (1, 2): [("o", 1)]})
    return at


def scalar_empties(item):
    return item[0] in "kq"


def tile_of(item):
    return item[1] * HALF_TILES + (item[2] if item[0] == "k" else KH)


def max_items(g):
    return [("max", g, h, qb, kh) for h in range(GH) for qb in range(QB) for kh in range(KH)]


class Unit:

    def __init__(self, index, layer, batch, w0, v0, bank, before, after):
        self.index, self.layer, self.batch = index, layer, batch
        self.w0, self.v0, self.bank, self.before, self.after = w0, v0, bank, before, after
        self.plan = {}
        side = side_items(before, after)
        for g in range(NG):
            ahead = (g + MAX_AHEAD) % NG
            todo = max_items(ahead) if g + MAX_AHEAD < NG or after is not None else []
            for kb in range(KB):
                self.plan[g, kb] = todo[kb * MAX_TILES:(kb + 1) * MAX_TILES] + side.get((g, kb), [])
            if g + 1 < NG or after is not None:
                self.plan[g, 1].append(("maxT", (g + 1) % NG))
        self.number_items([item for at in sorted(self.plan) for item in self.plan[at]])

    def number_items(self, order):
        self.order = order
        self.number = {item: n for n, item in enumerate(order)}
        mine = [item for item in order if not scalar_empties(item)]
        self.vector_number = {item: n for n, item in enumerate(mine)}

    def filled(self, item):
        return self.w0 + self.number[item] + 1

    def emptied(self, item):
        return self.v0 + self.vector_number[item] + 1

    def group(self, g, kind):
        first = MAX_AHEAD if kind == "max" else MAX_AHEAD - 1
        return self.index * NG + (g if g >= first else g + NG)

    def slot(self, item):
        return (self.bank + self.number[item]) % WORK_BANKS


class Prologue(Unit):

    def __init__(self):
        self.index, self.layer, self.batch, self.w0, self.v0, self.bank = -1, 0, -1, 0, 0, 0
        self.before, self.after = None, 0
        first = max_items(0)
        self.number_items([("k", 0, 0), ("k", 0, 1), ("q", 0)] + v_items(0)
                          + [("k", 1, 0), ("k", 1, 1)] + first[:24] + [("q", 1)] + first[24:]
                          + [("maxT", 0)] + max_items(1))


def plan_units():
    prologue = Prologue()
    w, v = len(prologue.order), len(prologue.vector_number)
    entries = []
    for layer in range(2):
        for batch in (0, 1, B - 1):
            before = None if layer == 0 and batch == 0 else (0 if batch == 0 else layer)
            after = (1 if layer == 0 else None) if batch == B - 1 else layer
            unit = Unit(0, layer, batch, 0, 0, 0, before, after)
            n, nv = len(unit.order), len(unit.vector_number)
            entries.append((layer, batch, w, n, v, nv, before, after))
            w += n * (B - 2 if batch == 1 else 1)
            v += nv * (B - 2 if batch == 1 else 1)
            assert batch != 1 or n % WORK_BANKS == 0
    return prologue, entries


def xattn_two_layers(nc, a, out):
    x_in = {0: a["x"], 1: nc.dram_tensor("layer0_out", (B, SQ, D), F32, kind="Internal").ap()}
    x_out = {0: x_in[1], 1: out}
    rden_rows = nc.dram_tensor("rden_rows", (2, GH, SQ), F32, kind="Internal").ap()
    prologue, entries = plan_units()

    def run_units(eng, body):
        for layer, batch, w, n, v, nv, before, after in entries:
            if batch == 1:
                with eng.Fori(1, B - 1) as i:
                    body(Unit(i + layer * B if layer else i, layer, i, (i - 1) * n + w, (i - 1) * nv + v,
                              w % WORK_BANKS, before, after))
            else:
                body(Unit(layer * B + batch, layer, batch, w, v, w % WORK_BANKS, before, after))

    with ExitStack() as ctx:
        def sb(name, shape, dt=F32):
            return ctx.enter_context(nc.sbuf_tensor(name, shape, dt))

        def sem(name):
            return ctx.enter_context(nc.semaphore(name))

        k6 = sb("k6", [P, H, SK], BF16)
        q6 = sb("q6", [P, H, SQ], BF16)
        vx = sb("vx", [P, NG, KB, GH, 2 * DH])
        probs = sb("probs", [P, 2, GH, SQ])
        ctx_t = sb("ctx_t", [P, NC, SK])
        x_t = sb("x_t", [P, NC, SQ])
        ctx_hl = sb("ctx_hl", [P, 2, NC, SK], F32R)
        x_hl = sb("x_hl", [P, 2, NC, SQ], F32R)
        full = sb("full", [P, 2, BANK])
        rest = sb("rest", [P, BANK])
        ks = sb("ks", [P, NC, 3, SK], BF16)
        qs = sb("qs", [P, NC, 3, SQ], BF16)
        vs = sb("vs", [P, KB, D])
        rows = sb("rows", [P, QB, D])
        o_raw = sb("o_raw", [P, 2, SQ])
        num = sb("num", [P, SQ])
        den = sb("den", [P, 2, GH * SQ // P])
        rden_s = sb("rden_s", [P, 2, GH * SQ // P])
        rden = sb("rden", [P, SQ])
        attn_t = sb("attn_t", [P, NC, SQ])
        res = sb("res", [P, QB, D])
        y = sb("y", [P, QB, D])
        negmax = sb("negmax", [P, KH, GH * QB])
        nm = sb("nm", [P, GH * QB])
        nm_parts = sb("nm_parts", [P, 2, GH * QB], BF16)
        nm_t = sb("nm_t", [2 * GH * QB, P], BF16)
        stats = sb("stats", [P, 2, QB, 6])
        mv = sb("mv", [P, 2, QB, 2])
        var = sb("var", [P, 2, QB])
        rstd = sb("rstd", [P, 2, QB])
        w_hl = sb("w_hl", [P, 2, 3, NC, D], F32R)
        w_t = sb("w_t", [P, 3, NC, D], F32R)
        wo = sb("wo", [P, 2, NC, D])
        absum = sb("absum", [P, 4])
        gam = sb("gam", [P, 4])
        thr = sb("thr", [P, 2, 4])
        tern = sb("tern", [P, NC, D])
        ones = sb("ones", [P, P])
        eye = sb("eye", [P, P])
        eyeb = sb("eyeb", [P, P], BF16)
        mhalf = sb("mhalf", [P, QB])
        bqk = sb("bqk", [P, 2, 2, NC])
        bv = sb("bv", [P, 2, D])
        bo = sb("bo", [P, 2, D])
        ln0 = sb("ln0", [P, 2, D])
        ln1 = sb("ln1", [P, 2, NC])

        ps = ctx.enter_context(nc.psum_tensor("ps", [P, 2, 2 * BANK], F32))
        pw = ctx.enter_context(nc.psum_tensor("pw", [P, WORK_BANKS, BANK], F32))
        po = ctx.enter_context(nc.psum_tensor("po", [P, BANK], F32))

        const_in = sem("const_in")
        w_in = {key: sem(f"w_in{key[0]}{key[1]}") for key in ((0, Q), (0, K), (0, V), (0, O), (1, Q))}
        w_split = sem("w_split")
        w_high = sem("w_high")
        ctx_high = sem("ctx_high")
        ctx_low = sem("ctx_low")
        x_high = sem("x_high")
        x_low = sem("x_low")
        ctx_in = [sem(f"ctx_in{kh}") for kh in range(KH)]
        x_t_in = sem("x_t_in")
        rows_in = sem("rows_in")
        res_in = sem("res_in")
        restacked = [sem(f"restacked{g}") for g in range(NG)]
        max_placed = sem("max_placed")
        o_moved = [sem(f"o_moved{p}") for p in range(2)]
        stored = sem("stored")
        consts_set = sem("consts_set")
        ones_set = sem("ones_set")
        abs_summed = sem("abs_summed")
        total_ready = sem("total_ready")
        quant_link = sem("quant_link")
        work_full = sem("work_full")
        work_done = sem("work_done")
        scores_full = sem("scores_full")
        probs_ready = sem("probs_ready")
        pv_done = sem("pv_done")
        o_copied = sem("o_copied")
        tile_taken = sem("tile_taken")
        tile_full = sem("tile_full")
        split_link = sem("split_link")
        split_done = sem("split_done")
        v_placed = sem("v_placed")
        max_link = sem("max_link")
        max_split = sem("max_split")
        rden_ready = sem("rden_ready")
        rden_stored = sem("rden_stored")
        rden_spread = sem("rden_spread")
        attn_ready = sem("attn_ready")
        resb_ready = sem("resb_ready")
        stat_link = sem("stat_link")
        var_ready = sem("var_ready")
        norm_link = sem("norm_link")
        fin_ready = sem("fin_ready")
        rstat_link = sem("rstat_link")
        rvar_ready = sem("rvar_ready")
        rnorm_link = sem("rnorm_link")
        rows_ready = sem("rows_ready")

        settled = {e: sem(f"settled_{e}") for e in ("sp", "dve", "pool")}

        def settle(eng, name):
            eng.sem_inc(settled[name], 1)

        def wait(eng, sem, count):
            if not isinstance(count, int) or count > 0:
                eng.wait_ge(sem, count)
                if eng is nc.sync and not isinstance(count, int):
                    settle(eng, "sp")

        block = ctx.enter_context(nc.Block())
        N_CONST = 9
        LAST = P // 2
        W_LAST = entries[-1][2] + entries[-1][3]
        V_LAST = entries[-1][4] + entries[-1][5]

        def split_parts(half, at):
            return ks[:, half, :, BANK * at:BANK * at + BANK] if at < KH else qs[:, half, :, :]

        def last_o(o):
            return ps[:, o, :].rearrange("p (j n) -> p j n", j=2)

        def low_ctx(eng, ops, n, kh):
            cols = slice(BANK * kh, BANK * kh + BANK)
            eng.wait_ge(ctx_high, n * KH + kh + 1)
            ops.tensor_tensor(ctx_hl[:, 1, :, cols], ctx_t[:, :, cols],
                              ctx_hl[:, 0, :, cols].bitcast(F32), ALU.subtract).then_inc(ctx_low, 1)

        def split(eng, ops, index, at):
            parts = split_parts(at // HALF_TILES, at % HALF_TILES)
            t = full[:, at % 2, :]
            n = index * TILES + at
            eng.wait_ge(tile_full, n + 1)
            wait(eng, split_done, n)
            ops.tensor_tensor(rest[:], t, parts[:, 0, :], ALU.subtract).then_inc(split_link, 1)
            eng.wait_ge(split_link, n * 2 + 1)
            if eng is nc.gpsimd:
                settle(eng, "pool")
            ops.tensor_copy(parts[:, 1, :], rest[:]).then_inc(split_link, 1)
            eng.wait_ge(split_link, n * 2 + 2)
            ops.tensor_tensor(parts[:, 2, :], rest[:], parts[:, 1, :], ALU.subtract).then_inc(split_done, 1)

        def raw(t, n):
            return t[:, 2 * n:2 * n + 2, :]

        raw_w = {(0, K): raw(res, 0), (0, Q): raw(res, 1), (0, V): raw(y, 0), (0, O): wo[:, 0],
                 (1, Q): raw(rows, 0), (1, K): raw(rows, 1), (1, V): raw(y, 1), (1, O): wo[:, 1]}

        def rows_of(dram, batch):
            return dram[batch].rearrange("(t p) d -> p t d", p=P)

        def load_weights(eng, layer, m):
            eng.dma_start(raw_w[layer, m], a["wts"][layer, m].rearrange("(c p) n -> p c n", p=P)
                          ).then_inc(w_in[(0, m) if layer == 0 else (1, Q)], 16)

        @block.sync
        def _(sp):
            def load_inputs(layer, batch):
                src = a["ctxT"][batch].rearrange("(c p) n -> p c n", p=P)
                for kh in range(KH):
                    cols = slice(BANK * kh, BANK * kh + BANK)
                    sp.dma_start(ctx_t[:, :, cols], src[:, :, cols]).then_inc(ctx_in[kh], 16)
                if layer == 0:
                    sp.dma_start(x_t[:], a["xT"][batch].rearrange("(c p) n -> p c n", p=P)).then_inc(x_t_in, 16)

            def restack(index, g):
                half, lane = g // 2, 64 * (g % 2)
                wait(sp, split_done, index * TILES + half * HALF_TILES + KH)
                for t in range(NT):
                    sp.dma_start(k6[DH * t:DH * t + DH, GH * g:GH * g + GH, :],
                                 ks[lane:lane + 64, half, K_PART[t], :]).then_inc(restacked[g], 16)
                wait(sp, split_done, index * TILES + (half + 1) * HALF_TILES)
                for t in range(NT):
                    sp.dma_start(q6[DH * t:DH * t + DH, GH * g:GH * g + GH, :],
                                 qs[lane:lane + 64, half, Q_PART[t], :]).then_inc(restacked[g], 16)

            def place_max(u, g):
                wait(sp, work_done, u.emptied(("maxT", g)))
                sp.dma_start(q6[ROWS:SROWS, GH * g:GH * g + GH, :], nm_t[:, :]).then_inc(max_placed, 16)

            def move_o(index, g):
                wait(sp, o_copied, index * NG + g + 1)
                wait(sp, attn_ready, index * NC + g // 2)
                lane = 64 * (g % 2)
                sp.dma_start(den[:, g % 2, :], o_raw[1:P:32, g % 2, :]).then_inc(o_moved[g % 2], 16)
                sp.dma_start(num[lane:lane + 64, :], o_raw[0:P:2, g % 2, :]).then_inc(o_moved[g % 2], 16)

            def spread_rden(index, g):
                lane, n = 64 * (g % 2), index * NG + g + 1
                wait(sp, rden_ready, n)
                sp.dma_start(rden_rows[g % 2], rden_s[:, g % 2, :]).then_inc(rden_stored, 16)
                wait(sp, rden_stored, n * 16)
                sp.dma_start(rden[lane:lane + 64, :],
                             rden_rows[g % 2].unsqueeze(1).to_broadcast([GH, DH, SQ])).then_inc(rden_spread, 16)

            def load_residual(index, layer, batch):
                if layer == 1:
                    wait(sp, stored, batch * 16 + 16)
                sp.dma_start(res[:], rows_of(x_in[layer], batch)).then_inc(res_in, 16)

            load_inputs(0, 0)
            load_weights(sp, 0, V)
            sp.dma_start(bqk[:].rearrange("p l k c -> p (l k c)"), a["bqk"]).then_inc(const_in, 16)
            sp.dma_start(eye[:], a["eye"]).then_inc(const_in, 16)
            for l in range(2):
                sp.dma_start(bv[:, l, :], a["bv"][l:l + 1, :].to_broadcast([P, D])).then_inc(const_in, 16)
                sp.dma_start(bo[:, l, :], a["bo"][l:l + 1, :].to_broadcast([P, D])).then_inc(const_in, 16)
                sp.dma_start(ln0[:, l, :], a["ln0"][l:l + 1, :].to_broadcast([P, D])).then_inc(const_in, 16)
            sp.dma_start(ln1[:].rearrange("p k c -> p (k c)"), a["ln1"]).then_inc(const_in, 16)
            load_weights(sp, 0, O)
            for m in (Q, K, V, O):
                load_weights(sp, 1, m)
            for g in range(NG):
                restack(0, g)
            place_max(prologue, 0)

            def unit(u):
                U = u.index
                wait(sp, work_done, u.v0)
                if u.after is not None:
                    next_batch = 0 if u.after != u.layer else u.batch + 1
                    if u.after == 1:
                        if u.layer == 1:
                            wait(sp, rows_ready, U - (B - 1))
                        wait(sp, stored, next_batch * 16 + 16)
                        sp.dma_start(rows[:], rows_of(x_in[1], next_batch)).then_inc(rows_in, 16)
                    load_inputs(u.after, next_batch)
                if u.before is not None:
                    last_batch = B - 1 if u.before != u.layer else u.batch - 1
                    move_o(U - 1, NG - 1)
                    load_residual(U - 1, u.before, last_batch)
                    wait(sp, scores_full, U * (NG * KB * 2))
                    restack(U, NG - 1)
                for g in range(NG):
                    if g > 0:
                        move_o(U, g - 1)
                    if g + 1 < NG or u.after is not None:
                        place_max(u, (g + 1) % NG)
                    if g > 0:
                        spread_rden(U, g - 1)
                        if u.after is not None:
                            wait(sp, scores_full, U * (NG * KB * 2) + g * KB * 2)
                            restack(U + 1, g - 1)
                    elif u.before is not None:
                        spread_rden(U - 1, NG - 1)
                if u.before is not None:
                    if u.before == 0:
                        wait(sp, fin_ready, U)
                    else:
                        wait(sp, work_done, u.emptied(("o", 1)))
                    sp.dma_start(rows_of(x_out[u.before], last_batch), y[:]).then_inc(stored, 16)
                    wait(sp, stored, U * 16)

            run_units(sp, unit)
            wait(sp, work_done, V_LAST)
            load_residual(2 * B - 1, 1, B - 1)
            wait(sp, o_copied, 2 * B * NG)
            sp.dma_start(rden[LAST:, :], o_raw[1:P:2, 1, :]).then_inc(o_moved[1], 16)
            sp.dma_start(num[LAST:, :], o_raw[0:P:2, 1, :]).then_inc(o_moved[1], 16)
            for o in range(2):
                wait(sp, work_done, V_LAST + o + 1)
                sp.dma_start(rows_of(out, B - 1)[:, 2 * o:2 * o + 2, :], y[:, 2 * o:2 * o + 2, :]
                             ).then_inc(stored, 16)
            wait(sp, stored, 2 * B * 16 + 16)

        @block.tensor
        def _(pe):
            def start_work(u, item):
                n = u.number[item] - WORK_BANKS
                if n < 0:
                    wait(pe, work_done, u.v0 + (n + 1))
                elif scalar_empties(u.order[n]):
                    pe.wait_ge(tile_taken, (u.index + 1) * TILES + tile_of(u.order[n]) + 1)
                else:
                    pe.wait_ge(work_done, u.emptied(u.order[n]))
                return pw[:, u.slot(item), :]

            def o_proj(dst, layer, o, chunks=range(NC)):
                for j in range(2):
                    qb = 2 * o + j
                    for c in chunks:
                        mm = nc.tensor.matmul(dst[:, j, 0:D], attn_t[:, c, P * qb:P * qb + P],
                                              wo[:, layer, c, :], start=(c == 0), stop=(c == NC - 1))
                return mm

            def products(layer, m, x):
                if layer == 1:
                    return [(w_t[:, m, c, :], x(part, c)) for c in range(NC) for part in (0, 1)]
                return [(w_hl[:, wp, m, c, :], x(xp, c)) for c in range(NC) for wp, xp in ((0, 0), (0, 1), (1, 0))]

            def work(u, item):
                dst = start_work(u, item)
                kind, nl, U = item[0], u.after, u.index
                if kind == "max":
                    _, g, h, qb, kh = item
                    if (h, qb, kh) == (0, 0, 0):
                        pe.wait_ge(restacked[g], (U + (g < MAX_AHEAD)) * (2 * NT * 16) + 2 * NT * 16)
                    s = GH * g + h
                    mm = nc.tensor.matmul(dst, q6[0:ROWS, s, P * qb:P * qb + P],
                                          k6[0:ROWS, s, BANK * kh:BANK * kh + BANK], start=True, stop=True)
                elif kind == "maxT":
                    pe.wait_ge(max_split, u.group(item[1], "maxT") + 1)
                    mm = nc.tensor.transpose(dst.bitcast(BF16)[0:2 * GH * QB, 0:P],
                                             nm_parts[:].rearrange("p k n -> p (k n)"), eyeb[:])
                elif kind == "xnT":
                    pe.wait_ge(rows_ready, U - (B - 1) + 1)
                    for qb in range(QB):
                        mm = nc.tensor.transpose(dst[:, P * qb:P * qb + P],
                                                 rows[:, qb, P * item[1]:P * item[1] + P], eye[:])
                elif kind == "k":
                    _, half, kh = item
                    if half == 0:
                        pe.wait_ge(ctx_low, (U + 1) * KH + kh + 1)
                    terms = products(nl, K, lambda part, c: ctx_hl[:, part, c, BANK * kh:BANK * kh + BANK])
                    for n, (w, x) in enumerate(terms):
                        mm = nc.tensor.matmul(dst, w[:, P * half:P * half + P], x,
                                              start=(n == 0), stop=(n == len(terms) - 1))
                elif kind == "q":
                    half = item[1]
                    if half == 0:
                        pe.wait_ge(x_low, U + 2)
                    terms = products(nl, Q, lambda part, c: x_hl[:, part, c, :])
                    for n, (w, x) in enumerate(terms):
                        mm = nc.tensor.matmul(dst, w[:, P * half:P * half + P], x,
                                              start=(n == 0), stop=(n == len(terms) - 1))
                elif kind == "v":
                    for j in range(item[2]):
                        kb = item[1] + j
                        terms = products(nl, V, lambda part, c: ctx_hl[:, part, c, P * kb:P * kb + P])
                        for n, (w, x) in enumerate(terms):
                            mm = nc.tensor.matmul(dst[:, D * j:D * j + D], x, w,
                                                  start=(n == 0), stop=(n == len(terms) - 1))
                else:
                    if item[1] == 0:
                        pe.wait_ge(attn_ready, U * NC)
                    mm = o_proj(dst.rearrange("p (j n) -> p j n", j=2), u.before, item[1])
                mm.then_inc(work_full, 1)

            def scores(u, g, kb, p):
                step = u.index * (NG * KB) + (g * KB + kb)
                if kb == 0 and p == 0:
                    pe.wait_ge(max_placed, (u.index * NG + g + 1) * 16)
                wait(pe, probs_ready, step * 2 + (p - 1))
                for j in range(2):
                    s = GH * g + 2 * p + j
                    mm = nc.tensor.matmul(ps[:, p, BANK * j:BANK * j + BANK],
                                          k6[0:SROWS, s, P * kb:P * kb + P], q6[0:SROWS, s, :],
                                          start=True, stop=True)
                mm.then_inc(scores_full, 1)

            def values(index, g, kb):
                if kb == 0:
                    pe.wait_ge(v_placed, index * NG + g + 1)
                    wait(pe, o_copied, index * NG + g)
                pe.wait_ge(probs_ready, index * (NG * KB * 2) + (g * KB + kb + 1) * 2)
                for h in range(GH):
                    mm = nc.tensor.matmul(po[32 * h:32 * h + 32, :], vx[:, g, kb, h, :],
                                          probs[:, kb % 2, h, :], start=(kb == 0), stop=(kb == KB - 1))
                mm.then_inc(pv_done, 1)

            for item in prologue.order:
                if item[1:] in ((0, 0), (0,)) or item[0] == "v":
                    wait(pe, w_split, {"k": 1, "q": 2, "v": 3}.get(item[0], 0))
                if item[0] == "maxT":
                    pe.wait_ge(consts_set, 1)
                work(prologue, item)
            pe.wait_ge(ones_set, 2)
            pe.wait_ge(abs_summed, 4)
            nc.tensor.matmul(po[:, 0:4], ones[:], absum[:], start=True, stop=True).then_inc(total_ready, 1)

            def unit(u):
                for g in range(NG):
                    for kb in range(KB):
                        items = u.plan[g, kb]
                        for item in items[0:1]:
                            work(u, item)
                        scores(u, g, kb, 0)
                        for item in items[1:2]:
                            work(u, item)
                        scores(u, g, kb, 1)
                        for item in items[2:3]:
                            work(u, item)
                        if kb > 0:
                            values(u.index, g, kb - 1)
                        elif g > 0:
                            values(u.index, g - 1, KB - 1)
                        elif u.before is not None:
                            values(u.index - 1, NG - 1, KB - 1)
                        for item in items[3:]:
                            work(u, item)

            run_units(pe, unit)
            values(2 * B - 1, NG - 1, KB - 1)
            pe.wait_ge(probs_ready, 2 * B * NG * KB * 2)
            pe.wait_ge(attn_ready, (2 * B - 1) * NC + 1)
            for o in range(2):
                o_proj(last_o(o), 1, o, (0,))
            for o in range(2):
                pe.wait_ge(attn_ready, (2 * B - 1) * NC + 1 + o + 1)
                o_proj(last_o(o), 1, o, (1,)).then_inc(work_full, 1)

        @block.scalar
        def _(act):
            load_weights(act, 0, K)
            load_weights(act, 0, Q)

            def high_ctx(n):
                for kh in range(KH):
                    act.wait_ge(ctx_in[kh], n * 16 + 16)
                    cols = slice(BANK * kh, BANK * kh + BANK)
                    nc.scalar.copy(ctx_hl[:, 0, :, cols], ctx_t[:, :, cols]).then_inc(ctx_high, 1)

            def high_x(n, layer, rows_turned):
                if layer == 0:
                    act.wait_ge(x_t_in, n * 16 + 16)
                else:
                    act.wait_ge(work_done, rows_turned)
                nc.scalar.copy(x_hl[:, 0], x_t[:]).then_inc(x_high, 1)

            def copy_o(index, g):
                act.wait_ge(pv_done, index * (NG * KB) + (g + 1) * KB)
                wait(act, o_moved[g % 2], (index * NC + g // 2) * 32)
                nc.scalar.copy(o_raw[:, g % 2, :], po[:]).then_inc(o_copied, 1)

            def project(u, item):
                half, at = item[1], tile_of(item)
                n = (u.index + 1) * TILES + at
                parts, src = split_parts(half, at % HALF_TILES), pw[:, u.slot(item), :]
                m = K if item[0] == "k" else Q
                bias = bqk[:, u.after, m, half:half + 1]
                scale = gam[:, m:m + 1] if u.after == 1 else 1.0
                act.wait_ge(work_full, u.filled(item))
                wait(act, split_done, n - 1)
                nc.scalar.activation(full[:, at % 2, :], src, ACT.Identity, bias=bias, scale=scale
                                     ).then_inc(tile_taken, 1)
                act.wait_ge(tile_taken, n + 1)
                nc.scalar.copy(parts[:, 0, :], full[:, at % 2, :]).then_inc(tile_full, 1)

            high_ctx(0)
            high_x(0, 0, None)
            act.wait_ge(const_in, N_CONST * 16)
            for item in prologue.order:
                if scalar_empties(item):
                    project(prologue, item)

            def unit(u):
                for g in range(NG):
                    for kb in range(KB):
                        step = u.index * (NG * KB) + (g * KB + kb)
                        wait(act, pv_done, step - 1)
                        for p in range(2):
                            act.wait_ge(scores_full, step * 2 + (p + 1))
                            nc.scalar.activation(probs[:, kb % 2, 2 * p:2 * p + 2, :].rearrange("p h n -> p (h n)"),
                                                 ps[:, p, :], ACT.Exp, scale=SCALE).then_inc(probs_ready, 1)
                        if kb == 0 and g > 0:
                            copy_o(u.index, g - 1)
                        elif kb == 0 and u.before is not None:
                            copy_o(u.index - 1, NG - 1)
                        if (g, kb) == (0, 2) and u.after is not None:
                            high_ctx(u.index + 1)
                        if (g, kb) == (1, 0) and u.after is not None:
                            high_x(u.index + 1, u.after, u.emptied(("xnT", NC - 1)) if u.after == 1 else None)
                        for item in u.plan[g, kb]:
                            if scalar_empties(item):
                                project(u, item)

            run_units(act, unit)
            copy_o(2 * B - 1, NG - 1)

        @block.vector
        def _(dve):
            def work(u, item):
                if scalar_empties(item):
                    return
                src = pw[:, u.slot(item), :]
                kind, nl, U, done = item[0], u.after, u.index, u.emptied(item)
                dve.wait_ge(work_full, u.filled(item))
                if kind == "max":
                    _, g, h, qb, kh = item
                    nc.vector.tensor_reduce(negmax[:, kh, QB * h + qb:QB * h + qb + 1], src, AX.X, ALU.max,
                                            negate=True).then_inc(work_done, 1)
                    if (h, qb, kh) == (GH - 1, QB - 1, KH - 1):
                        split_max(u, g, done)
                elif kind == "maxT":
                    wait(dve, max_placed, u.group(item[1], "maxT") * 16)
                    nc.vector.tensor_copy(nm_t[:], src.bitcast(BF16)[0:2 * GH * QB, 0:P]).then_inc(work_done, 1)
                elif kind == "xnT":
                    c = item[1]
                    nc.vector.tensor_scalar(x_t[:, c, :], src, ln1[:, 0, c:c + 1], ln1[:, 1, c:c + 1],
                                            ALU.mult, ALU.add).then_inc(work_done, 1)
                elif kind == "v":
                    if item[1] == 0:
                        wait(dve, v_placed, (U + 1) * NG)
                    n = item[2]
                    vals = src[:, 0:D * n].rearrange("p (j n) -> p j n", j=n)
                    bias = bv[:, nl:nl + 1, :].to_broadcast([P, n, D])
                    if nl == 0:
                        op = nc.vector.tensor_tensor(vs[:, item[1]:item[1] + n, :], vals, bias, ALU.add)
                    else:
                        op = nc.vector.scalar_tensor_tensor(out=vs[:, item[1]:item[1] + n, :], in0=vals,
                                                            scalar=gam[:, V:V + 1], in1=bias,
                                                            op0=ALU.mult, op1=ALU.add)
                    op.then_inc(work_done, 1)
                else:
                    empty_o(src.rearrange("p (j n) -> p j n", j=2), u.before, U, item[1])

            def empty_o(src, layer, index, o):
                if o == 0:
                    dve.wait_ge(resb_ready, index)
                    if layer == 0:
                        dve.wait_ge(v_placed, index * NG + NG)
                nc.vector.tensor_tensor(y[:, 2 * o:2 * o + 2, :], src[:, :, 0:D],
                                        res[:, 2 * o:2 * o + 2, :], ALU.add).then_inc(work_done, 1)

            def row_stats(t, s, qb, link):
                nc.vector.bn_stats(stats[:, s, qb, :], t[:, qb, :]).then_inc(link, 1)

            def variance(s, link, at, ready):
                dve.wait_ge(link, at + QB)
                settle(dve, "dve")
                for qb in range(QB):
                    last = nc.vector.bn_aggr(mv[:, s, qb, :], stats[:, s, qb, :])
                last.then_inc(link, 1)
                dve.wait_ge(link, at + QB + 1)
                nc.vector.tensor_scalar(var[:, s, :], mv[:, s, :, 1], LN_EPS, None, ALU.add).then_inc(ready, 1)

            def split_max(u, g, n):
                count = u.group(g, "max")
                dve.wait_ge(work_done, n)
                nc.vector.tensor_tensor(nm[:], negmax[:, 0, :], negmax[:, 1, :], ALU.min).then_inc(max_link, 1)
                dve.wait_ge(max_link, count * 2 + 1)
                nc.vector.tensor_copy(nm_parts[:, 0, :], nm[:]).then_inc(max_link, 1)
                dve.wait_ge(max_link, count * 2 + 2)
                nc.vector.tensor_tensor(nm_parts[:, 1, :], nm[:], nm_parts[:, 0, :],
                                        ALU.subtract).then_inc(max_split, 1)

            def invert_den(index, g):
                dve.wait_ge(o_moved[g % 2], (index * NC + g // 2 + 1) * 32)
                nc.vector.reciprocal(rden_s[:, g % 2, :], den[:, g % 2, :]).then_inc(rden_ready, 1)

            def normalize_attn(index, half):
                dve.wait_ge(rden_spread, (index * NC + half + 1) * 32)
                nc.vector.tensor_tensor(attn_t[:, half, :], num[:], rden[:], ALU.mult).then_inc(attn_ready, 1)

            def low_x(n, c):
                dve.wait_ge(x_high, n + 1)
                op = nc.vector.tensor_tensor(x_hl[:, 1, c, :], x_t[:, c, :], x_hl[:, 0, c, :].bitcast(F32),
                                             ALU.subtract)
                if c == NC - 1:
                    op.then_inc(x_low, 1)

            for n, m in enumerate((K, Q, V)):
                dve.wait_ge(w_in[0, m], 16)
                nc.vector.tensor_copy(w_hl[:, 0, m], raw_w[0, m]).then_inc(w_high, 1)
                dve.wait_ge(w_high, n + 1)
                nc.vector.tensor_tensor(w_hl[:, 1, m], raw_w[0, m], w_hl[:, 0, m].bitcast(F32), ALU.subtract
                                        ).then_inc(w_split, 1)
                if m == K:
                    for kh in range(KH):
                        low_ctx(dve, nc.vector, 0, kh)
                if m == Q:
                    for c in range(NC):
                        low_x(0, c)
            dve.wait_ge(const_in, N_CONST * 16)
            nc.vector.tensor_copy(eyeb[:], eye[:]).then_inc(consts_set, 1)
            nc.vector.memset(ones[:], 1.0)
            for item in prologue.order:
                if item == ("v", 0, 2):
                    for at in range(HALF_TILES):
                        split(dve, nc.vector, 0, at)
                work(prologue, item)
                if item == v_items(0)[-1]:
                    dve.wait_ge(w_in[1, Q], 4 * 16)
                    for m in range(4):
                        nc.vector.tensor_reduce(absum[:, m:m + 1], raw_w[1, m].rearrange("p c n -> p (c n)"),
                                                AX.X, ALU.add, apply_absolute_value=True
                                                ).then_inc(abs_summed, 1)

            dve.wait_ge(total_ready, 1)
            nc.vector.tensor_scalar(gam[:], po[:, 0:4], 1.0 / (D * D), None, ALU.mult).then_inc(quant_link, 1)
            dve.wait_ge(quant_link, 1)
            for s, sign in ((0, 0.5), (1, -0.5)):
                nc.vector.tensor_scalar(thr[:, s, :], gam[:], QUANT_EPS, sign, ALU.add, ALU.mult
                                        ).then_inc(quant_link, 1)

            def quantize(m):
                at = 3 + 2 * m
                w = raw_w[1, m]
                dve.wait_ge(quant_link, at)
                nc.vector.tensor_scalar(tern[:], w, thr[:, 1, m:m + 1], None, ALU.is_lt).then_inc(quant_link, 1)
                dve.wait_ge(quant_link, at + 1)
                nc.vector.scalar_tensor_tensor(out=w_t[:, m] if m < O else tern[:], in0=w,
                                               scalar=thr[:, 0, m:m + 1], in1=tern[:],
                                               op0=ALU.is_gt, op1=ALU.subtract).then_inc(quant_link, 1)
                if m == O:
                    dve.wait_ge(quant_link, at + 2)
                    nc.vector.scalar_tensor_tensor(out=tern[:], in0=tern[:], scalar=gam[:, m:m + 1], in1=w,
                                                   op0=ALU.mult, op1=ALU.subtract).then_inc(quant_link, 1)
                    dve.wait_ge(quant_link, at + 3)
                    nc.vector.tensor_tensor(w, w, tern[:], ALU.add).then_inc(quant_link, 1)

            def beside(u, g, kb, n):
                U, at = u.index, (g, kb)
                rows_from = u.after == 1 and U - (B - 1)
                if u.after == 1 and at in ((0, 1), (0, 2), (0, 3), (0, 4)) and n == 3:
                    if at == (0, 1):
                        dve.wait_ge(rows_in, rows_from * 16 + 16)
                    row_stats(rows, 1, kb - 1, rstat_link)
                if u.after == 1 and at == (0, 5) and n == 0:
                    variance(1, rstat_link, rows_from * 5, rvar_ready)
                if u.before == 0 and at in ((1, 3), (1, 4), (1, 5), (1, 6)) and n == 1:
                    if at == (1, 3):
                        dve.wait_ge(work_done, u.emptied(("o", 1)))
                    row_stats(y, 0, kb - 3, stat_link)
                if u.before == 0 and at == (1, 7) and n == 0:
                    variance(0, stat_link, (U - 1) * 5, var_ready)
                if kb == 2 and n == 1:
                    if g > 0:
                        invert_den(U, g - 1)
                    elif u.before is not None:
                        invert_den(U - 1, NG - 1)
                if at == (0, 6) and n == 1 and u.before is not None:
                    normalize_attn(U - 1, 1)
                if at == (2, 6) and n == 1:
                    normalize_attn(U, 0)
                if at == (1, 1) and u.after is not None and n % 2 == 1:
                    low_x(U + 1, n // 2)
                if kb == 5 and n == 3 and u.before is None:
                    quantize(g)

            def unit(u):
                for g in range(NG):
                    for kb in range(KB):
                        items = u.plan[g, kb]
                        for n in range(max(MAX_TILES, len(items))):
                            if n < len(items):
                                work(u, items[n])
                            if n < MAX_TILES:
                                beside(u, g, kb, n)

            run_units(dve, unit)
            dve.wait_ge(rden_spread, (2 * B * NG - 1) * 16)
            nc.vector.tensor_tensor(attn_t[0:LAST, 1, :], num[0:LAST, :], rden[0:LAST, :], ALU.mult)
            dve.wait_ge(o_moved[1], 2 * B * NC * 32)
            for o in range(2):
                q = slice(SQ // 2 * o, SQ // 2 * (o + 1))
                nc.vector.reciprocal(rden[LAST:, q], rden[LAST:, q]).then_inc(rden_ready, 1)
                dve.wait_ge(rden_ready, 2 * B * NG - 1 + o + 1)
                nc.vector.tensor_tensor(attn_t[LAST:, 1, q], num[LAST:, q], rden[LAST:, q], ALU.mult
                                        ).then_inc(attn_ready, 1)
            for o in range(2):
                dve.wait_ge(work_full, W_LAST + o + 1)
                empty_o(last_o(o), 1, 2 * B, o)

        @block.gpsimd
        def _(pool):
            def place_v(g):
                settle(pool, "pool")
                nc.gpsimd.tensor_copy(vx[:, g, :, :, 0:2 * DH:2],
                                      vs[:, :, GH * DH * g:GH * DH * (g + 1)].rearrange(
                                          "p k (h d) -> p k h d", h=GH)).then_inc(v_placed, 1)

            def add_bias(index, layer):
                pool.wait_ge(res_in, index * 16 + 16)
                nc.gpsimd.tensor_tensor(res[:], res[:], bo[:, layer:layer + 1, :].to_broadcast([P, QB, D]),
                                        ALU.add).then_inc(resb_ready, 1)

            def standardize(dst, src, s, link, at, ready=None):
                nc.gpsimd.tensor_tensor(rstd[:, s, :], var[:, s, :], mhalf[:], ALU.pow).then_inc(link, 1)
                pool.wait_ge(link, at + 1)
                settle(pool, "pool")
                for qb in range(QB):
                    last = nc.gpsimd.tensor_scalar(dst[:, qb, :], src[:, qb, :], mv[:, s, qb, 0:1],
                                                   rstd[:, s, qb:qb + 1], ALU.subtract, ALU.mult)
                last.then_inc(ready or link, 1)

            nc.gpsimd.memset(mhalf[:], -0.5)
            nc.gpsimd.memset(vx[:, :, :, :, 1:2 * DH:2], 1.0).then_inc(ones_set, 1)
            pool.wait_ge(ones_set, 1)
            nc.gpsimd.memset(k6[ROWS:SROWS, :, :], 1.0).then_inc(ones_set, 1)
            pool.wait_ge(const_in, N_CONST * 16)
            pool.wait_ge(ones_set, 2)
            pool.wait_ge(work_done, prologue.emptied(v_items(0)[-1]))
            for g in range(NG):
                place_v(g)
            for at in range(HALF_TILES, TILES):
                split(pool, nc.gpsimd, 0, at)

            def unit(u):
                U = u.index
                if u.before is not None:
                    pool.wait_ge(pv_done, U * (NG * KB))
                    place_v(NG - 1)
                    add_bias(U - 1, u.before)
                if u.after is not None:
                    for kh in range(KH):
                        low_ctx(pool, nc.gpsimd, U + 1, kh)
                if u.after == 1:
                    pool.wait_ge(rvar_ready, U - (B - 1) + 1)
                    standardize(rows, rows, 1, rnorm_link, U - (B - 1), rows_ready)
                if u.after is not None:
                    for at in range(HALF_TILES):
                        split(pool, nc.gpsimd, U + 1, at)
                if u.before == 0:
                    pool.wait_ge(var_ready, U)
                    standardize(y, y, 0, norm_link, (U - 1) * 3)
                    pool.wait_ge(norm_link, (U - 1) * 3 + 2)
                    nc.gpsimd.tensor_tensor(y[:], y[:], ln0[:, 0:1, :].to_broadcast([P, QB, D]), ALU.mult
                                            ).then_inc(norm_link, 1)
                    pool.wait_ge(norm_link, (U - 1) * 3 + 3)
                    nc.gpsimd.tensor_tensor(y[:], y[:], ln0[:, 1:2, :].to_broadcast([P, QB, D]), ALU.add
                                            ).then_inc(fin_ready, 1)

                if u.after is not None:
                    for at in range(HALF_TILES, TILES):
                        split(pool, nc.gpsimd, U + 1, at)
                    pool.wait_ge(work_done, u.emptied(v_items(u.after)[-1]))
                    for g in range(NG - 1):
                        pool.wait_ge(pv_done, U * (NG * KB) + (g + 1) * KB)
                        place_v(g)

            run_units(pool, unit)
            pool.wait_ge(work_done, V_LAST)
            add_bias(2 * B - 1, 1)


def kernel(**inputs):
    import numpy as np
    import concourse.bacc as _bacc
    from concourse import mybir as _mybir
    from concourse.bass_utils import run_bass_kernel_spmd as _run

    i = {k: np.asarray(v) for k, v in inputs.items()}
    perm = np.arange(D).reshape(NC, 2, GH, DH).transpose(0, 1, 3, 2).reshape(-1)
    w0 = i["L0_xattn_W_qkv"]
    b0 = i["L0_xattn_b_qkv"]
    wts = np.stack([
        np.stack([w0[:D][perm].T, w0[D:2 * D][perm].T, w0[2 * D:].T, i["L0_xattn_W_o"].T]),
        np.stack([i["L1_xattn_Wq"][perm].T, i["L1_xattn_Wk"][perm].T, i["L1_xattn_Wv"].T, i["L1_xattn_Wo"].T]),
    ])
    bqk = np.stack([b0[:D][perm], b0[D:2 * D][perm], i["L1_xattn_bq"][perm], i["L1_xattn_bk"][perm]])
    arrays = {
        "x": i["x"],
        "xT": i["x"].transpose(0, 2, 1),
        "ctxT": i["ctx_1024"].transpose(0, 2, 1),
        "wts": wts,
        "bqk": bqk.reshape(4 * NC, P).T,
        "bv": np.stack([b0[2 * D:], i["L1_xattn_bv"]]),
        "bo": np.stack([i["L0_xattn_b_o"], i["L1_xattn_bo"]]),
        "ln0": np.stack([i["L0_xattn_ln_gamma"], i["L0_xattn_ln_beta"]]),
        "ln1": np.stack([i["L1_xattn_ln_gamma"], i["L1_xattn_ln_beta"]]).reshape(2 * NC, P).T,
        "eye": np.eye(P, dtype=np.float32),
    }
    nc = _bacc.Bacc("TRN2", target_bir_lowering=False, num_devices=1)
    feeds, args = {}, {}
    for name, v in arrays.items():
        v = np.ascontiguousarray(v)
        feeds[f"in_{name}"] = v
        args[name] = nc.dram_tensor(f"in_{name}", v.shape, _mybir.dt.from_np(v.dtype), kind="ExternalInput").ap()
    out = nc.dram_tensor("out_0", (B, SQ, D), _mybir.dt.float32, kind="ExternalOutput").ap()
    xattn_two_layers(nc, args, out)
    r = _run(nc, [feeds], core_ids=[0])
    return r.results[0]["out_0"]
```
